# Optimizing a Trainium2 kernel written in Bass

```python
import numpy as np
import jax
import jax.numpy as jnp

def _softmax(x, axis=-1):
    return jax.nn.softmax(x, axis=axis)

def _gelu(x):
    return jax.nn.gelu(x, approximate=True)

def _silu(x):
    return jax.nn.silu(x)

def _sigmoid(x):
    return jax.nn.sigmoid(x)

def _layernorm(x, axis=-1, eps=1e-05):
    m = jnp.mean(x, axis=axis, keepdims=True)
    v = jnp.var(x, axis=axis, keepdims=True)
    return (x - m) / jnp.sqrt(v + eps)

def _scatter_add(tgt, idx, src, axis=0):
    return tgt.at[idx].add(src)

def _segment_sum(src, seg, n):
    return jax.ops.segment_sum(src, seg, n)
kernel_name = 'mk_adj_ffn_d1_adj_r2_59a5ae'

def setup_inputs(seed: int=0):
    np.random.seed(seed)
    _w = jnp.asarray

    def _rec_inputs():
        import jax
        import jax.numpy as jnp
        _gk = jax.random.key(seed)
        x = 7.22e-05 + 1 * jax.random.normal(jax.random.fold_in(_gk, 1), (32, 256, 256), jnp.float32)
        _a = jax.random.bernoulli(jax.random.fold_in(_gk, 2), 0.0625, (256, 256))
        _af = _a.astype(jnp.float32)
        adj = _af
        return (x, adj)
    x, adj = _rec_inputs()

    def _L0_gnn_setup():
        import jax, jax.numpy as jnp
        import numpy as np
        B, N, D = (8, 1024, 256)
        key = jax.random.key(seed)
        k1, k2, k3, k4, k5 = jax.random.split(key, 5)
        neuron_states = jax.random.normal(k1, (B, N, D), dtype=jnp.float32)
        adjacency = jax.random.randint(k2, (N, N), 0, 2).astype(jnp.float32)
        scale = 1.0 / np.sqrt(D)
        Wq = jax.random.normal(k3, (D, D), dtype=jnp.float32) * scale
        Wk = jax.random.normal(k4, (D, D), dtype=jnp.float32) * scale
        Wv = jax.random.normal(k5, (D, D), dtype=jnp.float32) * scale
        return {'neuron_states': neuron_states, 'adjacency': adjacency, 'Wq': Wq, 'Wk': Wk, 'Wv': Wv}
    _L0_gnn_all = _L0_gnn_setup()
    _L0_gnn_in = {k: v for k, v in _L0_gnn_all.items() if k in ('Wq', 'Wk', 'Wv')}
    del _L0_gnn_all

    def _L0_ffn_setup():
        import jax, jax.numpy as jnp
        import numpy as np
        D_MODEL = 256
        NUM_EXPERTS = 8
        TOP_K = 2
        FFN_MULT = 2
        HIDDEN = FFN_MULT * D_MODEL
        BATCH, SEQ = (4, 1024)
        key = jax.random.key(seed)
        k_x, k_g, k_bg, k_w1, k_w3, k_w2 = jax.random.split(key, 6)
        sd = 1.0 / np.sqrt(D_MODEL).astype(np.float32)
        sh = 1.0 / np.sqrt(HIDDEN).astype(np.float32)
        return {'x': jax.random.normal(k_x, (BATCH, SEQ, D_MODEL), dtype=jnp.float32), 'Wg': jax.random.normal(k_g, (D_MODEL, NUM_EXPERTS), dtype=jnp.float32) * sd, 'bg': jax.random.normal(k_bg, (NUM_EXPERTS,), dtype=jnp.float32) * 0.01, 'W1': jax.random.normal(k_w1, (NUM_EXPERTS, D_MODEL, HIDDEN), dtype=jnp.float32) * sd, 'W3': jax.random.normal(k_w3, (NUM_EXPERTS, D_MODEL, HIDDEN), dtype=jnp.float32) * sd, 'W2': jax.random.normal(k_w2, (NUM_EXPERTS, HIDDEN, D_MODEL), dtype=jnp.float32) * sh}
    _L0_ffn_all = _L0_ffn_setup()
    _L0_ffn_in = {k: v for k, v in _L0_ffn_all.items() if k in ('Wg', 'bg', 'W1', 'W3', 'W2')}
    del _L0_ffn_all
    return {'x': x, 'adj': adj, 'L0_gnn_Wq': _L0_gnn_in['Wq'], 'L0_gnn_Wk': _L0_gnn_in['Wk'], 'L0_gnn_Wv': _L0_gnn_in['Wv'], 'L0_ffn_Wg': _L0_ffn_in['Wg'], 'L0_ffn_bg': _L0_ffn_in['bg'], 'L0_ffn_W1': _L0_ffn_in['W1'], 'L0_ffn_W3': _L0_ffn_in['W3'], 'L0_ffn_W2': _L0_ffn_in['W2']}

def reference(x, adj, L0_gnn_Wq, L0_gnn_Wk, L0_gnn_Wv, L0_ffn_Wg, L0_ffn_bg, L0_ffn_W1, L0_ffn_W3, L0_ffn_W2):
    import jax
    import jax.numpy as jnp

    def _L0_gnn_ref(neuron_states, adjacency, Wq, Wk, Wv):
        import jax, jax.numpy as jnp
        import numpy as np
        B, N, D = (8, 1024, 256)
        q = jnp.einsum('bnd,ed->bne', neuron_states, Wq)
        k = jnp.einsum('bnd,ed->bne', neuron_states, Wk)
        v = jnp.einsum('bnd,ed->bne', neuron_states, Wv)
        rel = jnp.einsum('bnd,bmd->bnm', q, k)
        rel = adjacency.T[None, :, :] * rel
        rel = rel / jnp.linalg.norm(rel, axis=2, keepdims=True)
        return jnp.einsum('bnm,bmd->bnd', rel, v)

    def _L0_ffn_ref(x, Wg, bg, W1, W3, W2):
        import jax, jax.numpy as jnp
        import numpy as np
        D_MODEL = 256
        NUM_EXPERTS = 8
        TOP_K = 2
        FFN_MULT = 2
        HIDDEN = FFN_MULT * D_MODEL
        BATCH, SEQ = (4, 1024)
        B, S, D = x.shape
        E = Wg.shape[1]
        xt = x.reshape(-1, D)
        T = xt.shape[0]
        logits = xt @ Wg + bg
        top_vals, top_idx = jax.lax.top_k(logits, TOP_K)
        top_probs = jax.nn.softmax(top_vals, axis=-1)
        gate_w = jnp.zeros((T, E), dtype=xt.dtype).at[jnp.arange(T)[:, None], top_idx].add(top_probs)

        def body(y, expert):
            w1, w3, w2, g = expert
            h = jax.nn.silu(xt @ w1) * (xt @ w3)
            return (y + g[:, None] * (h @ w2), None)
        y0 = jnp.zeros_like(xt)
        y, _ = jax.lax.scan(body, y0, (W1, W3, W2, gate_w.T))
        return y.reshape(B, S, D)
    x = x + _L0_gnn_ref(_layernorm(x, axis=-1), adj, L0_gnn_Wq, L0_gnn_Wk, L0_gnn_Wv)
    x = x + _L0_ffn_ref(_layernorm(x, axis=-1), L0_ffn_Wg, L0_ffn_bg, L0_ffn_W1, L0_ffn_W3, L0_ffn_W2)
    return x

_drawn_inputs = setup_inputs


def setup_inputs(seed=0):
    import zlib

    import numpy as np

    out = dict(_drawn_inputs(seed))
    spreads = {}
    factors = {'L0_ffn_bg': 2.983}
    for name, (base, spread) in spreads.items():
        noise = np.random.default_rng([zlib.crc32(name.encode()), seed]).standard_normal(out[name].shape)
        drawn = base * np.exp(spread * noise) if base else spread * noise
        out[name] = jnp.asarray(drawn.astype(out[name].dtype))
    for name, factor in factors.items():
        out[name] = (out[name] * factor).astype(out[name].dtype)
    return out
```

```python
from contextlib import ExitStack

import concourse.bass as bass
from concourse import mybir

ALU = mybir.AluOpType
ACT = mybir.ActivationFunctionType
F32 = mybir.dt.float32
BF16 = mybir.dt.bfloat16
I32 = mybir.dt.int32
U32 = mybir.dt.uint32
AX_X = mybir.AxisListType.X

P = 128
EPS = 1e-5
TOP_K = 2
UNROLL = 4


class Index:

    def __init__(self, base, i=None, unroll=1):
        self.base, self.i, self.unroll = base, i, unroll

    def __add__(self, n):
        return Index(self.base + n, self.i, self.unroll)

    def __sub__(self, n):
        return self + (-n)

    def value(self, scale=1, plus=0):
        if self.i is None:
            return scale * self.base + plus
        return self.i * (scale * self.unroll) + (scale * self.base + plus)

    def before(self, ring=1):
        if self.i is None:
            return self.base // ring
        return self.i * (self.unroll // ring) + self.base // ring

    def place(self, ring):
        return self.base % ring

    def within(self, n):
        return self.i is not None or 0 <= self.base < n


def steps(eng, first, last, rolled_first, rolled_last, unroll, body):
    for k in range(first, rolled_first):
        body(Index(k))
    count = (rolled_last - rolled_first + 1) // unroll
    with eng.Fori(0, count) as i:
        for u in range(unroll):
            body(Index(rolled_first + u, i, unroll))
    for k in range(rolled_first + count * unroll, last + 1):
        body(Index(k))


def wait(eng, sem, count):
    if isinstance(count, int) and count <= 0:
        return
    eng.wait_ge(sem, count)


def hold(eng, held):
    eng.sem_inc(held, 1)


def graph_and_experts(nc, x, adj, w_q, w_k, w_v, w_gate, b_gate, w_1, w_3, w_2, out):
    BATCHES, NODES, D = x.shape
    EXPERTS, _, HID = w_1.shape
    TOKENS = BATCHES * NODES
    NT = NODES // P
    DC = D // P
    HC = HID // P
    TILES = TOKENS // P
    SLOTS = (TOP_K * TOKENS + EXPERTS * (P - 1)) // P
    ROWS = EXPERTS * TILES + (SLOTS - TOP_K * TILES)
    SPARE = ROWS * P
    TABLE = SPARE + P
    assert DC == NT == 2 and HID <= 512 and SLOTS > P and TABLE % P == 0
    S2 = SLOTS - P

    ctx = ExitStack()
    with ctx:
        def sb(name, shape, dt=F32):
            return ctx.enter_context(nc.sbuf_tensor(name, shape, dt))

        def sem(name):
            return ctx.enter_context(nc.semaphore(name))

        def sems(name, n):
            return [sem(f"{name}{i}") for i in range(n)]

        bank = [ctx.enter_context(nc.psum_tensor(f"bank{i}", [P, 512], F32)) for i in range(8)]
        tables = [nc.dram_tensor(f"table{j}", (TABLE, 2), F32, kind="Internal").ap() for j in range(TOP_K * NT)]
        tokens_dram = nc.dram_tensor("tokens", (TOKENS + P, D), F32, kind="Internal").ap()

        ident = sb("ident", [P, P])
        before = sb("before", [P, P], BF16)
        ones = sb("ones", [P, P], BF16)
        ones_col = sb("ones_col", [P, 1])
        zero_rows = sb("zero_rows", [P, D])
        half = sb("half", [P, NT])
        expert_no = sb("expert_no", [P, EXPERTS])
        token_no = sb("token_no", [P, TILES])
        spare_row = sb("spare_row", [P, 1])
        blank = sb("blank", [P, TABLE // P, 2])
        pad_id = sb("pad_id", [P, 1])
        adj_sb = sb("adj_sb", [P, NT, NODES])
        wq_sb = sb("wq_sb", [P, DC, D])
        wk_sb = sb("wk_sb", [P, DC, D])
        wv_sb = sb("wv_sb", [P, DC, D])
        a_t = sb("a_t", [P, DC, D])
        wv_t = sb("wv_t", [P, DC, D])
        wg_sb = sb("wg_sb", [P, DC, EXPERTS])
        bg_sb = sb("bg_sb", [P, EXPERTS])
        w1_sb = sb("w1_sb", [P, EXPERTS * DC * HID])
        w3_sb = sb("w3_sb", [P, EXPERTS * DC * HID])
        w2_sb = sb("w2_sb", [P, EXPERTS * HC * D])

        XR = 4
        x_in = sb("x_in", [P, XR, NT, D])
        part1 = sb("part1", [P, NT, 6])
        mean1 = sb("mean1", [P, 2, NT, 2])
        var1 = sb("var1", [P, 2, NT])
        rstd1 = sb("rstd1", [P, 2, NT])
        xn = sb("xn", [P, 2, NT, D])
        xn_t = sb("xn_t", [P, 2, DC, NODES])
        g_t = sb("g_t", [P, DC, NODES])
        v = sb("v", [P, NT, D])
        rel = sb("rel", [P, NT, NODES])
        rel_sq = sb("rel_sq", [P, NT, NODES])
        norm_sq = sb("norm_sq", [P, NT])
        norm_inv = sb("norm_inv", [P, NT])
        x1 = sb("x1", [P, 2, NT, D])
        part2 = sb("part2", [P, NT, 6])
        mean2 = sb("mean2", [P, NT, 2])
        var2 = sb("var2", [P, NT])
        rstd2 = sb("rstd2", [P, NT])
        xn2 = sb("xn2", [P, 2, NT, D])
        xn2_t = sb("xn2_t", [P, DC, NODES])

        logit = sb("logit", [P, NT, EXPERTS])
        top = sb("top", [P, NT, 8])
        top_at = sb("top_at", [P, NT, 8], U32)
        top_no = sb("top_no", [P, TOP_K, NT])
        chosen = sb("chosen", [P, TOP_K, NT, EXPERTS])
        either = sb("either", [P, NT, EXPERTS], BF16)
        margin = sb("margin", [P, NT])
        first_free = sb("first_free", [P, EXPERTS])
        start_row = sb("start_row", [P, EXPERTS])
        rank = sb("rank", [P, NT, EXPERTS])
        picked = sb("picked", [P, TOP_K * NT, EXPERTS])
        row = sb("row", [P, TOP_K * NT])
        row_u = sb("row_u", [P, 2, TOP_K * NT], U32)
        entry = sb("entry", [P, 2, TOP_K, NT, 2])

        count_i = sb("count_i", [P, EXPERTS], I32)
        slots_i = sb("slots_i", [P, EXPERTS], I32)
        slots_of = sb("slots_of", [P, EXPERTS])
        slots_end = sb("slots_end", [P, EXPERTS])
        all_ones = sb("all_ones", [P, EXPERTS])
        slot_gap = sb("slot_gap", [P, EXPERTS])
        slot_no = sb("slot_no", [P, 2])
        past = sb("past", [P, 2, EXPERTS])
        skipped = sb("skipped", [P, 2, EXPERTS])
        table_row = sb("table_row", [P, 2])
        table_row_u = sb("table_row_u", [P, 2], U32)
        slot_free = sb("slot_free", [1, SLOTS])
        past_free = sb("past_free", [1, SLOTS, EXPERTS])
        expert_f = sb("expert_f", [1, SLOTS])
        expert_of = sb("expert_of", [1, SLOTS], I32)
        by_slot1 = sb("by_slot1", [P, TOP_K * NT, P, 2])
        by_slot2 = sb("by_slot2", [S2, TOP_K * NT, P, 2])
        id_sum = sb("id_sum", [P, SLOTS])
        is_pad = sb("is_pad", [P, SLOTS])
        ids = sb("ids", [P, SLOTS], U32)
        gates = sb("gates", [P, SLOTS])

        gather_id = sb("gather_id", [P, 2], U32)
        scatter_id = sb("scatter_id", [P, 2], U32)
        xg = sb("xg", [P, 2, D])
        xg_t = sb("xg_t", [P, DC, P])
        silu = sb("silu", [P, HID])
        h = sb("h", [P, HID])
        h_t = sb("h_t", [P, HC, P])
        y = sb("y", [P, 2, D])

        held_dve = sem("held_dve")
        held_pool = sem("held_pool")
        x_loaded = sems("x_loaded", XR)
        graph_w_loaded = sem("graph_w_loaded")
        gate_w_loaded = sem("gate_w_loaded")
        expert_w_loaded = sem("expert_w_loaded")
        adj_loaded = sem("adj_loaded")
        ident_zero = sem("ident_zero")
        ident_made = sem("ident_made")
        before_made = sem("before_made")
        iotas_made = sem("iotas_made")
        zeros_made = sem("zeros_made")
        consts_made = sem("consts_made")
        blank_made = sem("blank_made")
        blank_stored = sem("blank_stored")
        spare_stored = sem("spare_stored")
        a_done = sem("a_done")
        wvt_done = sem("wvt_done")
        a_ready = sem("a_ready")
        wvt_ready = sem("wvt_ready")

        part1_ready = sem("part1_ready")
        mean1_ready = sem("mean1_ready")
        var1_ready = sem("var1_ready")
        rstd1_ready = sem("rstd1_ready")
        xn_ready = sem("xn_ready")
        xnt_done = sem("xnt_done")
        xnt_ready = sem("xnt_ready")
        g_done = sem("g_done")
        g_ready = sem("g_ready")
        v_done = sem("v_done")
        v_ready = sem("v_ready")
        rel_done = sem("rel_done")
        rel_ready = sem("rel_ready")
        relsq_ready = sem("relsq_ready")
        mix_done = sem("mix_done")
        norm_done = sem("norm_done")
        normsq_ready = sem("normsq_ready")
        norminv_ready = sem("norminv_ready")
        x1_ready = sem("x1_ready")
        x1_stored = sems("x1_stored", 2)
        part2_ready = sem("part2_ready")
        mean2_ready = sem("mean2_ready")
        var2_ready = sem("var2_ready")
        rstd2_ready = sem("rstd2_ready")
        xn2_ready = sem("xn2_ready")
        xn2_stored = sems("xn2_stored", 2)
        xn2t_done = sem("xn2t_done")
        xn2t_ready = sem("xn2t_ready")
        logit_done = sem("logit_done")
        logit_ready = sem("logit_ready")
        top_ready = sem("top_ready")
        topat_ready = sem("topat_ready")
        topno_ready = sem("topno_ready")
        chosen_ready = sem("chosen_ready")
        either_ready = sem("either_ready")
        margin_ready = sem("margin_ready")
        prefix_done = sem("prefix_done")
        rank_ready = sem("rank_ready")
        free_ready = sem("free_ready")
        picked_ready = sem("picked_ready")
        row_ready = sem("row_ready")
        rowu_ready = sem("rowu_ready")
        gate_ready = sem("gate_ready")
        id_ready = sem("id_ready")
        entries_stored = sems("entries_stored", TOP_K * NT)

        plan = sem("plan")
        tablerow_ready = sem("tablerow_ready")
        experts_ready = sem("experts_ready")
        byslot_loaded = sem("byslot_loaded")
        byslot_done = sem("byslot_done")
        ids_ready = sem("ids_ready")
        gates_ready = sem("gates_ready")

        gid_ready = sem("gid_ready")
        sid_ready = sem("sid_ready")
        xg_loaded = sems("xg_loaded", 2)
        xgt_done = sem("xgt_done")
        xgt_ready = sem("xgt_ready")
        up1_done = sem("up1_done")
        up3_done = sem("up3_done")
        silu_ready = sem("silu_ready")
        h_ready = sem("h_ready")
        ht_done = sem("ht_done")
        ht_ready = sem("ht_ready")
        down_done = sem("down_done")
        y_ready = sem("y_ready")
        y_added = sem("y_added")

        xnt_ps = bank[0][:, :].rearrange("p (c n) -> p c n", c=DC)
        g_ps = bank[1][:, :].rearrange("p (c n) -> p c n", c=DC)
        v_ps = bank[2][:, :].rearrange("p (t n) -> p t n", t=NT)
        rel_ps = bank[3][:, :].rearrange("p (t n) -> p t n", t=NT)
        mix_ps = bank[4][:, :].rearrange("p (t n) -> p t n", t=NT)
        xn2t_ps = bank[5][:, :].rearrange("p (c n) -> p c n", c=DC)
        norm_ps = bank[6][:, 0:NT]
        RE = NT * EXPERTS
        logit_ps = bank[7][:, 0:RE].rearrange("p (t e) -> p t e", t=NT)
        rank_ps = bank[7][:, 64:64 + RE].rearrange("p (t e) -> p t e", t=NT)
        count_ps = bank[7][:, 64 + RE:64 + RE + EXPERTS]
        byslot_ps = bank[7][:, 128:128 + 2 * SLOTS].rearrange("p (c s) -> p c s", c=2)
        up1_ps, up3_ps = bank[0], bank[1]
        ht_ps = bank[2][:, :].rearrange("p (c n) -> p c n", c=HC)
        xgt_ps = bank[3][:, 0:DC * P].rearrange("p (c n) -> p c n", c=DC)
        down_ps = bank[4][:, 0:D]

        x_rows = x.rearrange("b (t p) d -> (b t) p d", p=P)
        out_rows = out.rearrange("(r p) d -> r p d", p=P)
        token_rows = tokens_dram.rearrange("(r p) d -> r p d", p=P)

        def batch_rows(rows, b):
            return rows[bass.ds(b.value(NT), NT), :, :].rearrange("t p d -> p t d")

        LAG = 5
        G_ROLL = (LAG + 2, LAG + 1 + (BATCHES - LAG - 2) // UNROLL * UNROLL)

        def graph_steps(eng, body):
            steps(eng, 0, BATCHES - 1 + LAG, *G_ROLL, UNROLL, body)

        E_ROLL = (3, 3 + (SLOTS - 4) // 2 * 2 - 1)

        def expert_steps(eng, body):
            steps(eng, 0, SLOTS, *E_ROLL, 2, body)

        block = ctx.enter_context(nc.Block())

        @block.sync
        def _(sp):
            def load_x(b):
                sp.dma_start(x_in[:, b.place(XR)], batch_rows(x_rows, b)).then_inc(x_loaded[b.place(XR)], 16)

            load_x(Index(0))
            for w, to in ((w_q, wq_sb), (w_k, wk_sb), (w_v, wv_sb)):
                sp.dma_start(to[:, :, :], w.rearrange("(c p) d -> p c d", p=P)).then_inc(graph_w_loaded, 16)
            sp.dma_start(adj_sb[:, :, :], adj.rearrange("(t p) n -> p t n", p=P)).then_inc(adj_loaded, 16)
            for b in range(1, XR):
                load_x(Index(b))
            sp.dma_start(wg_sb[:, :, :], w_gate.rearrange("(c p) e -> p c e", p=P)).then_inc(gate_w_loaded, 16)
            sp.dma_start(bg_sb[:, :], b_gate.partition_broadcast(P)).then_inc(gate_w_loaded, 16)
            sp.wait_ge(zeros_made, 1)
            sp.dma_start(token_rows[TILES], zero_rows[:, :]).then_inc(spare_stored, 16)
            sp.dma_start(out_rows[TILES], zero_rows[:, :]).then_inc(spare_stored, 16)
            sp.wait_ge(blank_made, 1)
            for table in tables:
                sp.dma_start(table.rearrange("(p j) c -> p j c", p=P), blank[:, :, :]).then_inc(blank_stored, 16)

            def step(k):
                b = k - 3
                if b.within(BATCHES):
                    wait(sp, x1_ready, b.value(NT, NT))
                    sp.dma_start(batch_rows(out_rows, b), x1[:, b.place(2)]).then_inc(x1_stored[b.place(2)], 16)
                nxt = k + 1
                if nxt.within(BATCHES) and (nxt.i is not None or nxt.base >= XR):
                    load_x(nxt)
                if b.within(BATCHES):
                    wait(sp, xn2_ready, b.value(NT, NT))
                    sp.dma_start(batch_rows(token_rows, b), xn2[:, b.place(2)]).then_inc(xn2_stored[b.place(2)], 16)

            graph_steps(sp, step)

        @block.gpsimd
        def _(pool):
            pool.memset(ident[:, :], 0.0).then_inc(ident_zero, 1)
            pool.memset(before[:, :], 1.0).then_inc(ident_zero, 1)
            pool.wait_ge(ident_zero, 2)
            pool.affine_select(out=ident[:, :], in_=ident[:, :], compare_op=ALU.not_equal, fill=1.0, base=0,
                               pattern=[[-1, P]], channel_multiplier=1).then_inc(ident_made, 1)
            pool.affine_select(out=before[:, :], in_=before[:, :], compare_op=ALU.is_gt, fill=0.0, base=0,
                               pattern=[[1, P]], channel_multiplier=-1).then_inc(before_made, 1)
            pool.memset(zero_rows[:, :], 0.0).then_inc(zeros_made, 1)
            pool.memset(half[:, :], -0.5).then_inc(iotas_made, 1)
            pool.iota(expert_no[:, :], [[1, EXPERTS]], base=0, channel_multiplier=0,
                      allow_small_or_imprecise_dtypes=True).then_inc(iotas_made, 1)
            pool.iota(start_row[:, :], [[TOKENS, EXPERTS]], base=-SPARE, channel_multiplier=-1,
                      allow_small_or_imprecise_dtypes=True).then_inc(iotas_made, 1)
            pool.iota(spare_row[:, :], [[0, 1]], base=SPARE, channel_multiplier=1,
                      allow_small_or_imprecise_dtypes=True).then_inc(iotas_made, 1)
            pool.iota(token_no[:, :], [[P, TILES]], base=1, channel_multiplier=1,
                      allow_small_or_imprecise_dtypes=True).then_inc(iotas_made, 1)
            pool.iota(slot_no[:, :], [[P, 2]], base=0, channel_multiplier=1,
                      allow_small_or_imprecise_dtypes=True).then_inc(iotas_made, 1)
            pool.iota(slot_free[:, :], [[1, SLOTS]], base=0, channel_multiplier=0,
                      allow_small_or_imprecise_dtypes=True).then_inc(iotas_made, 1)
            pool.iota(pad_id[:, :], [[0, 1]], base=TOKENS + 1, channel_multiplier=1,
                      allow_small_or_imprecise_dtypes=True).then_inc(iotas_made, 1)

            def step(k):
                b = k - 3
                if b.within(BATCHES):
                    wait(pool, normsq_ready, b.value(1, 1))
                    wait(pool, x1_ready, b.value(NT))
                    pool.tensor_tensor(norm_inv[:, :], norm_sq[:, :], half[:, :], ALU.pow).then_inc(norminv_ready, 1)
                if k.within(BATCHES):
                    if k.i is None and k.base == 0:
                        pool.wait_ge(iotas_made, 8)
                    wait(pool, var1_ready, k.value(1, 1))
                    wait(pool, xn_ready, (k - 1).value(NT))
                    pool.tensor_tensor(rstd1[:, k.place(2)], var1[:, k.place(2)], half[:, :],
                                       ALU.pow).then_inc(rstd1_ready, 1)
                if b.within(BATCHES):
                    wait(pool, var2_ready, b.value(1, 1))
                    wait(pool, xn2_ready, b.value(NT))
                    pool.tensor_tensor(rstd2[:, :], var2[:, :], half[:, :], ALU.pow).then_inc(rstd2_ready, 1)
                r = k - 5
                if r.within(BATCHES):
                    q = r.place(2)
                    for stored in entries_stored:
                        wait(pool, stored, (r - 1).value(16))
                    for kk in range(TOP_K):
                        pool.tensor_copy(entry[:, q, kk, :, 0], token_no[:, bass.ds(r.value(NT), NT)]) \
                            .then_inc(id_ready, 1)
                    wait(pool, id_ready, r.value(TOP_K, TOP_K))
                    wait(pool, gate_ready, r.value(TOP_K, TOP_K))
                    wait(pool, rowu_ready, r.value(1, 1))
                    if r.i is None and r.base == 0:
                        pool.wait_ge(blank_stored, 16 * len(tables))
                    for kk in range(TOP_K):
                        for t in range(NT):
                            j = kk * NT + t
                            wait(pool, entries_stored[j], r.value(16))
                            hold(pool, held_pool)
                            pool.indirect_dma_start(
                                tables[j][:, :], bass.IndirectOffsetOnAxis(row_u[:, q, j:j + 1], 0),
                                entry[:, q, kk, t, :], None).then_inc(entries_stored[j], 16)

            graph_steps(pool, step)

            pool.wait_ge(tablerow_ready, 1)
            for j, table in enumerate(tables):
                pool.wait_ge(entries_stored[j], 16 * BATCHES)
                by_row = table.rearrange("(r p) c -> r (p c)", p=P)
                for n, to in ((P, by_slot1), (S2, by_slot2)):
                    at = table_row_u[0:n, 0:1] if n == P else table_row_u[0:n, 1:2]
                    pool.indirect_dma_start(to[:, j].rearrange("s p c -> s (p c)"), None, by_row,
                                            bass.IndirectOffsetOnAxis(at, 0)).then_inc(byslot_loaded, 16)
            for q in range(2):
                pool.wait_ge(xn2_stored[q], BATCHES // 2 * 16)
                pool.wait_ge(x1_stored[q], BATCHES // 2 * 16)
            pool.wait_ge(spare_stored, 32)
            pool.wait_ge(ids_ready, 1)

            def gather(s):
                q = s.place(2)
                wait(pool, xgt_done, (s - 1).value())
                pool.tensor_copy(gather_id[:, q:q + 1], ids[:, bass.ds(s.value(), 1)]).then_inc(gid_ready, 1)
                wait(pool, gid_ready, s.value(1, 1))
                hold(pool, held_pool)
                pool.indirect_dma_start(xg[:, q, :], None, tokens_dram[:, :],
                                        bass.IndirectOffsetOnAxis(gather_id[:, q:q + 1], 0)) \
                    .then_inc(xg_loaded[q], 16)

            def add(s):
                q = s.place(2)
                wait(pool, y_added, s.value(16))
                pool.tensor_copy(scatter_id[:, q:q + 1], ids[:, bass.ds(s.value(), 1)]).then_inc(sid_ready, 1)
                wait(pool, sid_ready, s.value(1, 1))
                wait(pool, y_ready, s.value(1, 1))
                hold(pool, held_pool)
                pool.indirect_dma_start(out[:, :], bass.IndirectOffsetOnAxis(scatter_id[:, q:q + 1], 0),
                                        y[:, q, :], None, compute_op=ALU.add).then_inc(y_added, 16)

            gather(Index(0))
            gather(Index(1))

            def expert_step(s):
                if (s + 2).within(SLOTS):
                    gather(s + 2)
                if (s - 1).within(SLOTS):
                    add(s - 1)

            steps(pool, 0, SLOTS, 2, 2 + (SLOTS - 4) // 2 * 2 - 1, 2, expert_step)
            pool.wait_ge(y_added, 16 * SLOTS)

        @block.scalar
        def _(act):
            for e in range(EXPERTS):
                for w, to, c in ((w_1, w1_sb, DC), (w_3, w3_sb, DC), (w_2, w2_sb, HC)):
                    n = c * w.shape[2]
                    act.dma_start(to[:, e * n:(e + 1) * n].rearrange("p (c n) -> p c n", c=c),
                                  w[e].rearrange("(c p) n -> p c n", p=P)).then_inc(expert_w_loaded, 16)
            act.wait_ge(a_done, 1)
            act.copy(a_t[:, :, :], g_ps).then_inc(a_ready, 1)
            act.wait_ge(wvt_done, 1)
            act.copy(wv_t[:, :, :], v_ps).then_inc(wvt_ready, 1)

            def step(k):
                b = k - 1
                if b.within(BATCHES):
                    wait(act, xnt_done, b.value(1, 1))
                    wait(act, rel_done, (b - 1).value())
                    act.copy(xn_t[:, b.place(2)], xnt_ps).then_inc(xnt_ready, 1)
                b = k - 2
                if b.within(BATCHES):
                    wait(act, g_done, b.value(1, 1))
                    wait(act, rel_done, b.value())
                    act.copy(g_t[:, :, :], g_ps).then_inc(g_ready, 1)
                    wait(act, v_done, b.value(1, 1))
                    wait(act, mix_done, b.value())
                    act.copy(v[:, :, :], v_ps).then_inc(v_ready, 1)
                r = k - 5
                if r.within(BATCHES):
                    q = r.place(2)
                    wait(act, margin_ready, r.value(1, 1))
                    wait(act, id_ready, r.value(TOP_K, TOP_K))
                    for kk, sign in ((0, 1.0), (1, -1.0)):
                        act.activation(entry[:, q, kk, :, 1], margin[:, :], ACT.Sigmoid,
                                       scale=sign).then_inc(gate_ready, 1)
                b = k - 4
                if b.within(BATCHES):
                    wait(act, xn2t_done, b.value(1, 1))
                    wait(act, logit_done, b.value())
                    act.copy(xn2_t[:, :, :], xn2t_ps).then_inc(xn2t_ready, 1)
                b = k - 2
                if b.within(BATCHES):
                    wait(act, rel_ready, b.value(1, 1))
                    wait(act, norm_done, b.value())
                    act.activation(rel_sq[:, :, :], rel[:, :, :], ACT.Square).then_inc(relsq_ready, 1)

            graph_steps(act, step)
            act.wait_ge(byslot_done, 1)
            act.copy(gates[:, :], byslot_ps[:, 1, :]).then_inc(gates_ready, 1)
            act.wait_ge(gates_ready, 1)

            def transposed(s):
                wait(act, xgt_done, s.value(1, 1))
                act.copy(xg_t[:, :, :], xgt_ps).then_inc(xgt_ready, 1)

            transposed(Index(0))

            def expert_step(s):
                if s.within(SLOTS):
                    wait(act, up1_done, s.value(1, 1))
                    wait(act, h_ready, s.value())
                    act.activation(silu[:, :], up1_ps[:, :], ACT.Silu).then_inc(silu_ready, 1)
                if (s + 1).within(SLOTS):
                    transposed(s + 1)
                d = s - 1
                if d.within(SLOTS):
                    wait(act, down_done, d.value(1, 1))
                    wait(act, y_added, (d - 1).value(16))
                    act.activation(y[:, d.place(2), :], down_ps, ACT.Copy,
                                   scale=gates[:, bass.ds(d.value(), 1)]).then_inc(y_ready, 1)

            expert_steps(act, expert_step)

        @block.vector
        def _(dve):
            dve.memset(ones[:, :], 1.0).then_inc(consts_made, 1)
            dve.memset(ones_col[:, :], 1.0).then_inc(consts_made, 1)
            dve.memset(all_ones[:, :], 1.0).then_inc(consts_made, 1)
            dve.memset(blank[:, :, :], 0.0).then_inc(blank_made, 1)
            dve.wait_ge(iotas_made, 8)
            dve.tensor_copy(first_free[:, :], start_row[:, :]).then_inc(free_ready, 1)
            def step(k):
                b = k - 1
                if b.within(BATCHES):
                    q = b.place(2)
                    wait(dve, rstd1_ready, b.value(1, 1))
                    wait(dve, xnt_done, (b - 1).value())
                    for t in range(NT):
                        dve.tensor_scalar(xn[:, q, t, :], x_in[:, b.place(XR), t, :], mean1[:, q, t, 0:1],
                                          rstd1[:, q, t:t + 1], ALU.subtract, ALU.mult).then_inc(xn_ready, 1)
                r = k - 5
                if r.within(BATCHES):
                    if r.i is None and r.base == 0:
                        dve.wait_ge(gate_w_loaded, 32)
                    wait(dve, logit_done, r.value(1, 1))
                    dve.tensor_tensor(logit[:, :, :], logit_ps,
                                      bg_sb[:, :].unsqueeze(1).to_broadcast([P, NT, EXPERTS]),
                                      ALU.add).then_inc(logit_ready, 1)
                    wait(dve, logit_ready, r.value(1, 1))
                    hold(dve, held_dve)
                    for t in range(NT):
                        dve.max(top[:, t, :], logit[:, t, :]).then_inc(top_ready, 1)
                    wait(dve, top_ready, r.value(NT, NT))
                    hold(dve, held_dve)
                    for t in range(NT):
                        dve.max_index(top_at[:, t, :], top[:, t, :], logit[:, t, :]).then_inc(topat_ready, 1)
                    wait(dve, gate_ready, r.value(TOP_K))
                    dve.tensor_tensor(margin[:, :], top[:, :, 0], top[:, :, 1], ALU.subtract) \
                        .then_inc(margin_ready, 1)
                    wait(dve, topat_ready, r.value(NT, NT))
                    dve.tensor_copy(top_no[:, :, :], top_at[:, :, 0:TOP_K].rearrange("p t k -> p k t")) \
                        .then_inc(topno_ready, 1)
                    wait(dve, topno_ready, r.value(1, 1))
                    for kk in range(TOP_K):
                        dve.tensor_tensor(chosen[:, kk], expert_no[:, :].unsqueeze(1).to_broadcast([P, NT, EXPERTS]),
                                          top_no[:, kk, :].unsqueeze(2).to_broadcast([P, NT, EXPERTS]),
                                          ALU.is_equal).then_inc(chosen_ready, 1)
                    wait(dve, chosen_ready, r.value(TOP_K, TOP_K))
                    wait(dve, prefix_done, r.value())
                    dve.tensor_tensor(either[:, :, :], chosen[:, 0], chosen[:, 1], ALU.add).then_inc(either_ready, 1)
                b = k - 3
                if b.within(BATCHES):
                    q = b.place(2)
                    wait(dve, norminv_ready, b.value(1, 1))
                    wait(dve, mix_done, b.value(1, 1))
                    wait(dve, x1_stored[q], b.before(2) * 16)
                    for t in range(NT):
                        dve.scalar_tensor_tensor(x1[:, q, t, :], mix_ps[:, t, :], norm_inv[:, t:t + 1],
                                                 x_in[:, b.place(XR), t, :], ALU.mult, ALU.add) \
                            .then_inc(x1_ready, 1)
                    wait(dve, x1_ready, b.value(NT, NT))
                    for t in range(NT):
                        dve.bn_stats(part2[:, t, :], x1[:, q, t, :]).then_inc(part2_ready, 1)
                    wait(dve, part2_ready, b.value(NT, NT))
                    hold(dve, held_dve)
                    for t in range(NT):
                        dve.bn_aggr(mean2[:, t, :], part2[:, t, :]).then_inc(mean2_ready, 1)
                    wait(dve, mean2_ready, b.value(NT, NT))
                    wait(dve, rstd2_ready, b.value())
                    dve.tensor_scalar(var2[:, :], mean2[:, :, 1], EPS, None, ALU.add).then_inc(var2_ready, 1)
                if k.within(BATCHES):
                    q = k.place(2)
                    wait(dve, x_loaded[k.place(XR)], k.before(XR) * 16 + 16)
                    for t in range(NT):
                        dve.bn_stats(part1[:, t, :], x_in[:, k.place(XR), t, :]).then_inc(part1_ready, 1)
                    wait(dve, part1_ready, k.value(NT, NT))
                    hold(dve, held_dve)
                    for t in range(NT):
                        dve.bn_aggr(mean1[:, q, t, :], part1[:, t, :]).then_inc(mean1_ready, 1)
                    wait(dve, mean1_ready, k.value(NT, NT))
                    dve.tensor_scalar(var1[:, q, :], mean1[:, q, :, 1], EPS, None, ALU.add).then_inc(var1_ready, 1)
                if r.within(BATCHES):
                    wait(dve, prefix_done, r.value(1, 1))
                    wait(dve, free_ready, r.value(1, 1))
                    dve.tensor_tensor(rank[:, :, :], rank_ps,
                                      first_free[:, :].unsqueeze(1).to_broadcast([P, NT, EXPERTS]),
                                      ALU.add).then_inc(rank_ready, 1)
                    wait(dve, rank_ready, r.value(1, 1))
                    dve.tensor_tensor(first_free[:, :], count_ps, first_free[:, :], ALU.add).then_inc(free_ready, 1)
                    for kk in range(TOP_K):
                        dve.tensor_tensor(picked[:, kk * NT:(kk + 1) * NT, :], chosen[:, kk], rank[:, :, :],
                                          ALU.mult).then_inc(picked_ready, 1)
                    wait(dve, picked_ready, r.value(TOP_K, TOP_K))
                    dve.tensor_reduce(row[:, :], picked[:, :, :], AX_X, ALU.add).then_inc(row_ready, 1)
                    wait(dve, row_ready, r.value(1, 1))
                    wait(dve, id_ready, r.value(TOP_K, TOP_K))
                    dve.tensor_scalar(row_u[:, r.place(2), :], row[:, :], spare_row[:, 0:1], None,
                                      ALU.add).then_inc(rowu_ready, 1)
                m = k - 2
                if m.within(BATCHES):
                    if m.i is None and m.base == 0:
                        dve.wait_ge(adj_loaded, 16)
                    wait(dve, rel_done, m.value(1, 1))
                    wait(dve, mix_done, m.value())
                    wait(dve, relsq_ready, m.value())
                    dve.tensor_tensor(rel[:, :, :], rel_ps, adj_sb[:, :, :], ALU.mult).then_inc(rel_ready, 1)
                if b.within(BATCHES):
                    q = b.place(2)
                    wait(dve, rstd2_ready, b.value(1, 1))
                    wait(dve, xn2_stored[q], b.before(2) * 16)
                    wait(dve, xn2t_done, (b - 1).value())
                    for t in range(NT):
                        dve.tensor_scalar(xn2[:, q, t, :], x1[:, q, t, :], mean2[:, t, 0:1], rstd2[:, t:t + 1],
                                          ALU.subtract, ALU.mult).then_inc(xn2_ready, 1)
                if m.within(BATCHES):
                    wait(dve, norm_done, m.value(1, 1))
                    wait(dve, norminv_ready, m.value())
                    dve.tensor_copy(norm_sq[:, :], norm_ps).then_inc(normsq_ready, 1)

            graph_steps(dve, step)

            n = 0
            dve.wait_ge(free_ready, BATCHES + 1)
            dve.tensor_tensor(count_i[:, :], first_free[:, :], start_row[:, :], ALU.subtract).then_inc(plan, 1)
            dve.wait_ge(plan, n + 1)
            dve.tensor_scalar(count_i[:, :], count_i[:, :], P - 1, None, ALU.add).then_inc(plan, 1)
            dve.wait_ge(plan, n + 2)
            dve.tensor_scalar(slots_i[:, :], count_i[:, :], P.bit_length() - 1, None,
                              ALU.logical_shift_right).then_inc(plan, 1)
            dve.wait_ge(plan, n + 3)
            dve.tensor_copy(slots_of[:, :], slots_i[:, :]).then_inc(plan, 1)
            dve.wait_ge(plan, n + 4)
            dve.tensor_tensor_scan(slots_end[:, :], all_ones[:, :], slots_of[:, :], 0.0, ALU.mult, ALU.add) \
                .then_inc(plan, 1)
            dve.tensor_scalar(slot_gap[:, :], slots_of[:, :], -1.0, float(TILES), ALU.mult, ALU.add).then_inc(plan, 1)
            dve.wait_ge(plan, n + 6)
            for j in range(2):
                dve.tensor_scalar(past[:, j, :], slots_end[:, :], slot_no[:, j:j + 1], None, ALU.is_le) \
                    .then_inc(plan, 1)
            dve.wait_ge(plan, n + 8)
            dve.tensor_tensor(skipped[:, :, :], past[:, :, :],
                              slot_gap[:, :].unsqueeze(1).to_broadcast([P, 2, EXPERTS]), ALU.mult).then_inc(plan, 1)
            dve.wait_ge(plan, n + 9)
            dve.tensor_reduce(table_row[:, :], skipped[:, :, :], AX_X, ALU.add).then_inc(plan, 1)
            dve.wait_ge(plan, n + 10)
            dve.tensor_tensor(table_row_u[:, :], table_row[:, :], slot_no[:, :], ALU.add).then_inc(tablerow_ready, 1)
            dve.tensor_tensor(past_free[:, :, :], slot_free[:, :].unsqueeze(2).to_broadcast([1, SLOTS, EXPERTS]),
                              slots_end[0:1, :].unsqueeze(1).to_broadcast([1, SLOTS, EXPERTS]),
                              ALU.is_ge).then_inc(plan, 1)
            dve.wait_ge(plan, n + 11)
            dve.tensor_reduce(expert_f[:, :], past_free[:, :, :], AX_X, ALU.add).then_inc(plan, 1)
            dve.wait_ge(plan, n + 12)
            dve.tensor_scalar(expert_of[:, :], expert_f[:, :], float(EXPERTS - 1), None, ALU.min) \
                .then_inc(experts_ready, 1)
            dve.wait_ge(byslot_done, 1)
            dve.wait_ge(gates_ready, 1)
            dve.tensor_copy(id_sum[:, :], byslot_ps[:, 0, :]).then_inc(plan, 1)
            dve.wait_ge(plan, n + 13)
            dve.tensor_scalar(is_pad[:, :], id_sum[:, :], 0.0, pad_id[:, 0:1], ALU.is_equal, ALU.mult) \
                .then_inc(plan, 1)
            dve.wait_ge(plan, n + 14)
            dve.scalar_tensor_tensor(ids[:, :], id_sum[:, :], -1.0, is_pad[:, :], ALU.add, ALU.add) \
                .then_inc(ids_ready, 1)

            def expert_step(s):
                d = s - 1
                if d.within(SLOTS):
                    wait(dve, ht_done, d.value(1, 1))
                    wait(dve, down_done, d.value())
                    dve.tensor_copy(h_t[:, :, :], ht_ps).then_inc(ht_ready, 1)
                if s.within(SLOTS):
                    wait(dve, up3_done, s.value(1, 1))
                    wait(dve, silu_ready, s.value(1, 1))
                    wait(dve, ht_done, s.value())
                    dve.tensor_tensor(h[:, :], up3_ps[:, :], silu[:, :], ALU.mult).then_inc(h_ready, 1)

            expert_steps(dve, expert_step)

        @block.tensor
        def _(pe):
            pe.wait_ge(ident_made, 1)
            pe.wait_ge(graph_w_loaded, 48)
            for c in range(DC):
                for e in range(DC):
                    mm = pe.matmul(g_ps[:, c, :], wq_sb[:, e, c * P:(c + 1) * P], wk_sb[:, e, :],
                                   start=(e == 0), stop=(e == DC - 1))
            mm.then_inc(a_done, 1)
            for c in range(DC):
                for e in range(DC):
                    mm = pe.transpose(v_ps[:, c, e * P:(e + 1) * P], wv_sb[:, e, c * P:(c + 1) * P], ident[:, :])
            mm.then_inc(wvt_done, 1)

            def step(k):
                b = k - 1
                if b.within(BATCHES):
                    wait(pe, xn_ready, b.value(NT, NT))
                    wait(pe, xnt_ready, b.value())
                    for t in range(NT):
                        for c in range(DC):
                            mm = pe.transpose(xnt_ps[:, c, t * P:(t + 1) * P],
                                              xn[:, b.place(2), t, c * P:(c + 1) * P], ident[:, :])
                    mm.then_inc(xnt_done, 1)
                m = k - 2
                if m.within(BATCHES):
                    xt = xn_t[:, m.place(2)]
                    if m.i is None and m.base == 0:
                        pe.wait_ge(a_ready, 1)
                        pe.wait_ge(wvt_ready, 1)
                    wait(pe, xnt_ready, m.value(1, 1))
                    wait(pe, g_ready, m.value())
                    for c in range(DC):
                        for e in range(DC):
                            mm = pe.matmul(g_ps[:, c, :], a_t[:, e, c * P:(c + 1) * P], xt[:, e, :],
                                           start=(e == 0), stop=(e == DC - 1))
                    mm.then_inc(g_done, 1)
                    wait(pe, v_ready, m.value())
                    for t in range(NT):
                        for e in range(DC):
                            mm = pe.matmul(v_ps[:, t, :], xt[:, e, t * P:(t + 1) * P], wv_t[:, e, :],
                                           start=(e == 0), stop=(e == DC - 1))
                    mm.then_inc(v_done, 1)
                r = k - 5
                if r.within(BATCHES):
                    if r.i is None and r.base == 0:
                        pe.wait_ge(before_made, 1)
                        pe.wait_ge(consts_made, 2)
                    wait(pe, either_ready, r.value(1, 1))
                    pe.matmul(rank_ps[:, 0, :], before[:, :], either[:, 0, :], start=True, stop=True)
                    pe.matmul(rank_ps[:, 1, :], before[:, :], either[:, 1, :], start=True, stop=False)
                    pe.matmul(rank_ps[:, 1, :], ones[:, :], either[:, 0, :], start=False, stop=True)
                    pe.matmul(count_ps, ones[:, :], either[:, 0, :], start=True, stop=False)
                    pe.matmul(count_ps, ones[:, :], either[:, 1, :], start=False, stop=True).then_inc(prefix_done, 1)
                b = k - 4
                if b.within(BATCHES):
                    wait(pe, xn2_ready, b.value(NT, NT))
                    wait(pe, xn2t_ready, b.value())
                    for t in range(NT):
                        for c in range(DC):
                            mm = pe.transpose(xn2t_ps[:, c, t * P:(t + 1) * P],
                                              xn2[:, b.place(2), t, c * P:(c + 1) * P], ident[:, :])
                    mm.then_inc(xn2t_done, 1)
                if m.within(BATCHES):
                    wait(pe, g_ready, m.value(1, 1))
                    wait(pe, rel_ready, m.value())
                    for t in range(NT):
                        for e in range(DC):
                            mm = pe.matmul(rel_ps[:, t, :], xt[:, e, t * P:(t + 1) * P], g_t[:, e, :],
                                           start=(e == 0), stop=(e == DC - 1))
                    mm.then_inc(rel_done, 1)
                if b.within(BATCHES):
                    if b.i is None and b.base == 0:
                        pe.wait_ge(gate_w_loaded, 32)
                    wait(pe, xn2t_ready, b.value(1, 1))
                    wait(pe, rank_ready, b.value())
                    wait(pe, free_ready, b.value(1, 1))
                    for t in range(NT):
                        for e in range(DC):
                            mm = pe.matmul(logit_ps[:, t, :], xn2_t[:, e, t * P:(t + 1) * P], wg_sb[:, e, :],
                                           start=(e == 0), stop=(e == DC - 1))
                    mm.then_inc(logit_done, 1)
                if m.within(BATCHES):
                    wait(pe, rel_ready, m.value(1, 1))
                    wait(pe, v_ready, m.value(1, 1))
                    wait(pe, x1_ready, m.value(NT))
                    for t in range(NT):
                        for e in range(NT):
                            mm = pe.matmul(mix_ps[:, t, :], rel[:, e, t * P:(t + 1) * P], v[:, e, :],
                                           start=(e == 0), stop=(e == NT - 1))
                    mm.then_inc(mix_done, 1)
                    wait(pe, relsq_ready, m.value(1, 1))
                    wait(pe, normsq_ready, m.value())
                    for t in range(NT):
                        for e in range(NT):
                            mm = pe.matmul(norm_ps[:, t:t + 1], rel_sq[:, e, t * P:(t + 1) * P], ones_col[:, :],
                                           start=(e == 0), stop=(e == NT - 1))
                    mm.then_inc(norm_done, 1)

            graph_steps(pe, step)

            pe.wait_ge(byslot_loaded, 32 * len(tables))
            pe.wait_ge(rank_ready, BATCHES)
            pe.wait_ge(free_ready, BATCHES + 1)
            for c in range(2):
                for n, at, of in ((P, 0, by_slot1), (S2, P, by_slot2)):
                    for j in range(len(tables)):
                        mm = pe.matmul(byslot_ps[:, c, at:at + n], of[:, j, :, c], ident[0:n, 0:n],
                                       start=(j == 0), stop=(j == len(tables) - 1))
            mm.then_inc(byslot_done, 1)
            pe.wait_ge(experts_ready, 1)
            pe.wait_ge(expert_w_loaded, 16 * 3 * EXPERTS)
            pe.wait_ge(rel_ready, BATCHES)
            pe.wait_ge(v_ready, BATCHES)
            pe.wait_ge(x1_ready, BATCHES * NT)

            def expert(s):
                return pe.value_load(expert_of[0:1, bass.ds(s.value(), 1)], min_val=0, max_val=EXPERTS - 1)

            def transpose_x(s):
                wait(pe, xg_loaded[s.place(2)], s.before(2) * 16 + 16)
                wait(pe, xgt_ready, s.value())
                for c in range(DC):
                    mm = pe.transpose(xgt_ps[:, c, :], xg[:, s.place(2), c * P:(c + 1) * P], ident[:, :])
                mm.then_inc(xgt_done, 1)

            transpose_x(Index(0))

            def expert_step(s):
                d = s - 1
                if s.within(SLOTS):
                    w = expert(s) * (DC * HID)
                    wait(pe, xgt_ready, s.value(1, 1))
                    wait(pe, silu_ready, s.value())
                    for c in range(DC):
                        mm = pe.matmul(up1_ps[:, :], xg_t[:, c, :], w1_sb[:, bass.ds(w + c * HID, HID)],
                                       start=(c == 0), stop=(c == DC - 1))
                    mm.then_inc(up1_done, 1)
                if d.within(SLOTS):
                    wait(pe, h_ready, d.value(1, 1))
                    wait(pe, ht_ready, d.value())
                    for c in range(HC):
                        mm = pe.transpose(ht_ps[:, c, :], h[:, c * P:(c + 1) * P], ident[:, :])
                    mm.then_inc(ht_done, 1)
                if s.within(SLOTS):
                    wait(pe, h_ready, s.value())
                    for c in range(DC):
                        mm = pe.matmul(up3_ps[:, :], xg_t[:, c, :], w3_sb[:, bass.ds(w + c * HID, HID)],
                                       start=(c == 0), stop=(c == DC - 1))
                    mm.then_inc(up3_done, 1)
                if (s + 1).within(SLOTS):
                    transpose_x(s + 1)
                if d.within(SLOTS):
                    w = expert(d) * (HC * D)
                    wait(pe, ht_ready, d.value(1, 1))
                    wait(pe, y_ready, d.value())
                    for c in range(HC):
                        mm = pe.matmul(down_ps, h_t[:, c, :], w2_sb[:, bass.ds(w + c * D, D)],
                                       start=(c == 0), stop=(c == HC - 1))
                    mm.then_inc(down_done, 1)

            expert_steps(pe, expert_step)


def kernel(x, adj, L0_gnn_Wq, L0_gnn_Wk, L0_gnn_Wv, L0_ffn_Wg, L0_ffn_bg, L0_ffn_W1, L0_ffn_W3, L0_ffn_W2):
    import numpy as np
    import concourse.bacc as bacc
    from concourse.bass_utils import run_bass_kernel_spmd

    given = {"x": x, "adj": adj, "w_q": L0_gnn_Wq, "w_k": L0_gnn_Wk, "w_v": L0_gnn_Wv, "w_gate": L0_ffn_Wg,
             "b_gate": L0_ffn_bg, "w_1": L0_ffn_W1, "w_3": L0_ffn_W3, "w_2": L0_ffn_W2}
    nc = bacc.Bacc("TRN2", target_bir_lowering=False, num_devices=1)
    arrays, args = {}, []
    for name, a in given.items():
        a = np.ascontiguousarray(a)
        arrays[f"in_{name}"] = a
        args.append(nc.dram_tensor(f"in_{name}", a.shape, mybir.dt.from_np(a.dtype), kind="ExternalInput").ap())
    batches, nodes, d = x.shape
    out = nc.dram_tensor("out", (batches * nodes + P, d), F32, kind="ExternalOutput").ap()
    graph_and_experts(nc, *args, out)
    r = run_bass_kernel_spmd(nc, [arrays], core_ids=[0])
    return r.results[0]["out"][:batches * nodes].reshape(batches, nodes, d)
```

```python
from contextlib import ExitStack

import concourse.bass as bass
from concourse import mybir

ALU = mybir.AluOpType
ACT = mybir.ActivationFunctionType
F32 = mybir.dt.float32
F32R = mybir.dt.float32r
BF16 = mybir.dt.bfloat16
I32 = mybir.dt.int32
U32 = mybir.dt.uint32
AX_X = mybir.AxisListType.X

P = 128
EPS = 1e-5
TOP_K = 2
UNROLL = 4


class Index:

    def __init__(self, base, i=None, unroll=1):
        self.base, self.i, self.unroll = base, i, unroll

    def __add__(self, n):
        return Index(self.base + n, self.i, self.unroll)

    def __sub__(self, n):
        return self + (-n)

    def value(self, scale=1, plus=0):
        if self.i is None:
            return scale * self.base + plus
        return self.i * (scale * self.unroll) + (scale * self.base + plus)

    def before(self, ring=1):
        if self.i is None:
            return self.base // ring
        return self.i * (self.unroll // ring) + self.base // ring

    def place(self, ring):
        return self.base % ring

    def within(self, n):
        return self.i is not None or 0 <= self.base < n


def steps(eng, first, last, rolled_first, rolled_last, unroll, body):
    for k in range(first, rolled_first):
        body(Index(k))
    count = (rolled_last - rolled_first + 1) // unroll
    with eng.Fori(0, count) as i:
        for u in range(unroll):
            body(Index(rolled_first + u, i, unroll))
    for k in range(rolled_first + count * unroll, last + 1):
        body(Index(k))


def wait(eng, sem, count):
    if isinstance(count, int) and count <= 0:
        return
    eng.wait_ge(sem, count)


def hold(eng, held):
    eng.sem_inc(held, 1)


def graph_and_experts(nc, x, adj, w_q, w_k, w_v, w_gate, b_gate, w_1, w_3, w_2, out):
    BATCHES, NODES, D = x.shape
    EXPERTS, _, HID = w_1.shape
    TOKENS = BATCHES * NODES
    NT = NODES // P
    DC = D // P
    HC = HID // P
    TILES = TOKENS // P
    SLOTS = (TOP_K * TOKENS + EXPERTS * (P - 1)) // P
    ROWS = EXPERTS * TILES + (SLOTS - TOP_K * TILES)
    SPARE = ROWS * P
    TABLE = SPARE + P
    assert DC == NT == 2 and HID <= 512 and SLOTS > P and TABLE % P == 0
    S2 = SLOTS - P
    WEIGHTS = DC * HID
    assert WEIGHTS == HC * D

    ctx = ExitStack()
    with ctx:
        def sb(name, shape, dt=F32):
            return ctx.enter_context(nc.sbuf_tensor(name, shape, dt))

        def sem(name):
            return ctx.enter_context(nc.semaphore(name))

        def sems(name, n):
            return [sem(f"{name}{i}") for i in range(n)]

        bank = [ctx.enter_context(nc.psum_tensor(f"bank{i}", [P, 512], F32)) for i in range(8)]
        tables = [nc.dram_tensor(f"table{j}", (TABLE, 2), F32, kind="Internal").ap() for j in range(TOP_K * NT)]
        tokens_dram = nc.dram_tensor("tokens", (TOKENS + P, D), F32, kind="Internal").ap()

        ALIGN = 32
        first_byte = -(-nc.sbuf_base // ALIGN) * ALIGN

        class Area:

            def __init__(self, start, size):
                self.at, self.end = start, start + size

            def __call__(self, name, shape, dt=F32):
                n = mybir.dt.size(dt)
                for m in shape[1:]:
                    n *= m
                t = nc.alloc_sbuf_tensor_at(name, shape, dt, offset=self.at)
                self.at += -(-n // ALIGN) * ALIGN
                assert self.at <= self.end, (name, self.at - self.end)
                return t

        UP = EXPERTS * DC * HID * 4
        DOWN = EXPERTS * HC * D * 4
        LAST = DOWN // EXPERTS
        SLOT = (2 * D + 2 * DC * P + HID + 2 * HC * P + 2 * D) * 4
        up_area = Area(first_byte, 4 * UP)
        down_at = up_area.end
        slot_at = down_at + 2 * DOWN
        keep = Area(slot_at + SLOT, nc.sbuf_usable_end - slot_at - SLOT)

        def weights(name, area, n):
            hi = area(f"{name}_hi", [P, n], F32R)
            at = area.at
            lo = area(f"{name}_lo", [P, n], F32R)
            raw = Area(at, n * 4)(f"{name}_raw", [P, n])
            return hi, lo, raw

        w1_hi, w1_lo, w1_raw = weights("w1", up_area, UP // 4)
        w3_hi, w3_lo, w3_raw = weights("w3", up_area, UP // 4)
        w2_hi, w2_lo, w2_raw = weights("w2", Area(down_at, 2 * DOWN), DOWN // 4)

        area = Area(slot_at, SLOT)
        xg = area("xg", [P, 2, D])
        xgt_hi = area("xgt_hi", [P, DC, P], F32R)
        xgt_lo = area("xgt_lo", [P, DC, P], F32R)
        h = area("h", [P, HID])
        ht_hi = area("ht_hi", [P, HC, P], F32R)
        late_at = area.at
        ht_lo = area("ht_lo", [P, HC, P], F32R)
        y = area("y", [P, 2, D])
        area = Area(slot_at, late_at - slot_at)
        by_slot1 = area("by_slot1", [P, TOP_K * NT, P, 2])
        by_slot2 = area("by_slot2", [S2, TOP_K * NT, P, 2])
        area = Area(late_at, slot_at + SLOT - late_at)
        id_sum = area("id_sum", [P, SLOTS])
        is_pad = area("is_pad", [P, SLOTS])
        slot_free = area("slot_free", [1, SLOTS])
        expert_f = area("expert_f", [1, SLOTS])
        area = Area(slot_at, late_at - slot_at)
        zero_rows = area("zero_rows", [P, D])
        blank = area("blank", [P, TABLE // P, 2])

        ident = keep("ident", [P, P])
        ids = keep("ids", [P, SLOTS], U32)
        gates = keep("gates", [P, SLOTS])
        weights_at = keep("weights_at", [1, SLOTS], I32)
        gather_id = keep("gather_id", [P, 2], U32)
        scatter_id = keep("scatter_id", [P, 2], U32)
        first_free = keep("first_free", [P, EXPERTS])
        start_row = keep("start_row", [P, EXPERTS])
        entry = keep("entry", [P, 2, TOP_K, NT, 2])
        row_u = keep("row_u", [P, 2, TOP_K * NT], U32)
        pad_id = keep("pad_id", [P, 1])
        slot_no = keep("slot_no", [P, 2])
        all_ones = keep("all_ones", [P, EXPERTS])
        count_i = keep("count_i", [P, EXPERTS], I32)
        slots_i = keep("slots_i", [P, EXPERTS], I32)
        slots_of = keep("slots_of", [P, EXPERTS])
        slots_end = keep("slots_end", [P, EXPERTS])
        slot_gap = keep("slot_gap", [P, EXPERTS])
        past = keep("past", [P, 2, EXPERTS])
        skipped = keep("skipped", [P, 2, EXPERTS])
        table_row = keep("table_row", [P, 2])
        table_row_u = keep("table_row_u", [P, 2], U32)

        XR = 4
        area = Area(down_at, DOWN - LAST)
        x_in = area("x_in", [P, XR, NT, D])
        xn = area("xn", [P, 2, NT, D])
        xn_t = area("xn_t", [P, 2, DC, NODES])
        xnt_hi = area("xnt_hi", [P, 2, DC, NODES], F32R)
        xnt_lo = area("xnt_lo", [P, 2, DC, NODES], F32R)
        area = Area(down_at + DOWN, DOWN - LAST)
        g_t = area("g_t", [P, DC, NODES])
        v = area("v", [P, NT, D])
        rel = area("rel", [P, NT, NODES])
        rel_sq = area("rel_sq", [P, NT, NODES])
        x1 = area("x1", [P, 2, NT, D])
        adj_sb = area("adj_sb", [P, NT, NODES])
        at_hi = area("at_hi", [P, DC, D], F32R)
        at_lo = area("at_lo", [P, DC, D], F32R)
        wvt_hi = area("wvt_hi", [P, DC, D], F32R)
        wvt_lo = area("wvt_lo", [P, DC, D], F32R)
        over = Area(area.at - (4 * DC * D + NT * NODES + 2 * NT * D + 4 * NT * NODES) * 4, 4 * NT * NODES * 4)
        wq_sb = over("wq_sb", [P, DC, D])
        wk_sb = over("wk_sb", [P, DC, D])
        wv_sb = over("wv_sb", [P, DC, D])
        small = area
        half = small("half", [P, NT])
        part1 = small("part1", [P, NT, 6])
        mean1 = small("mean1", [P, 2, NT, 2])
        var1 = small("var1", [P, 2, NT])
        rstd1 = small("rstd1", [P, 2, NT])
        shift1 = small("shift1", [P, 2, NT])
        norm_sq = small("norm_sq", [P, NT])
        norm_inv = small("norm_inv", [P, NT])
        part2 = small("part2", [P, NT, 6])
        mean2 = small("mean2", [P, NT, 2])
        var2 = small("var2", [P, NT])
        rstd2 = small("rstd2", [P, NT])
        ones_col = small("ones_col", [P, 1])

        area = Area(down_at + DOWN - LAST, LAST)
        xn2 = area("xn2", [P, 2, NT, D])
        area = Area(down_at + 2 * DOWN - LAST, LAST)
        xn2_t = area("xn2_t", [P, DC, NODES])
        wg_sb = area("wg_sb", [P, DC, EXPERTS])
        bg_sb = area("bg_sb", [P, EXPERTS])
        before = area("before", [P, P], BF16)
        ones = area("ones", [P, P], BF16)
        token_no = area("token_no", [P, TILES])
        expert_no = area("expert_no", [P, EXPERTS])
        spare_row = area("spare_row", [P, 1])
        logit = area("logit", [P, NT, EXPERTS])
        top = area("top", [P, NT, 8])
        top_at = area("top_at", [P, NT, 8], U32)
        top_no = area("top_no", [P, TOP_K, NT])
        chosen = area("chosen", [P, TOP_K, NT, EXPERTS])
        either = area("either", [P, NT, EXPERTS], BF16)
        margin = area("margin", [P, NT])
        rank = area("rank", [P, NT, EXPERTS])
        picked = area("picked", [P, TOP_K * NT, EXPERTS])
        row = area("row", [P, TOP_K * NT])

        held_dve = sem("held_dve")
        held_pool = sem("held_pool")
        x_loaded = sems("x_loaded", XR)
        graph_w_loaded = sem("graph_w_loaded")
        gate_w_loaded = sem("gate_w_loaded")
        up_loaded = sems("up_loaded", 2 * EXPERTS)
        down_loaded = sems("down_loaded", EXPERTS)
        up_hi_ready = sem("up_hi_ready")
        up_lo_ready = sem("up_lo_ready")
        down_hi_ready = sem("down_hi_ready")
        down_lo_ready = sem("down_lo_ready")
        adj_loaded = sem("adj_loaded")
        ident_zero = sem("ident_zero")
        ident_made = sem("ident_made")
        before_made = sem("before_made")
        iotas_made = sem("iotas_made")
        zeros_made = sem("zeros_made")
        consts_made = sem("consts_made")
        blank_made = sem("blank_made")
        blank_stored = sem("blank_stored")
        spare_stored = sem("spare_stored")
        a_done = sem("a_done")
        wvt_done = sem("wvt_done")
        a_hi_ready = sem("a_hi_ready")
        a_lo_ready = sem("a_lo_ready")
        wvt_hi_ready = sem("wvt_hi_ready")
        wvt_lo_ready = sem("wvt_lo_ready")

        part1_ready = sem("part1_ready")
        mean1_ready = sem("mean1_ready")
        var1_ready = sem("var1_ready")
        rstd1_ready = sem("rstd1_ready")
        xn_ready = sem("xn_ready")
        xnt_done = sem("xnt_done")
        xnt_ready = sem("xnt_ready")
        xnthi_ready = sem("xnthi_ready")
        xntlo_ready = sem("xntlo_ready")
        shift1_ready = sem("shift1_ready")
        g_done = sem("g_done")
        g_ready = sem("g_ready")
        v_done = sem("v_done")
        v_ready = sem("v_ready")
        rel_done = sem("rel_done")
        rel_ready = sem("rel_ready")
        relsq_ready = sem("relsq_ready")
        mix_done = sem("mix_done")
        norm_done = sem("norm_done")
        normsq_ready = sem("normsq_ready")
        norminv_ready = sem("norminv_ready")
        x1_ready = sem("x1_ready")
        x1_stored = sems("x1_stored", 2)
        part2_ready = sem("part2_ready")
        mean2_ready = sem("mean2_ready")
        var2_ready = sem("var2_ready")
        rstd2_ready = sem("rstd2_ready")
        xn2_ready = sem("xn2_ready")
        xn2_stored = sems("xn2_stored", 2)
        xn2t_done = sem("xn2t_done")
        xn2t_ready = sem("xn2t_ready")
        logit_done = sem("logit_done")
        logit_ready = sem("logit_ready")
        top_ready = sem("top_ready")
        topat_ready = sem("topat_ready")
        topno_ready = sem("topno_ready")
        chosen_ready = sem("chosen_ready")
        either_ready = sem("either_ready")
        margin_ready = sem("margin_ready")
        prefix_done = sem("prefix_done")
        rank_ready = sem("rank_ready")
        free_ready = sem("free_ready")
        picked_ready = sem("picked_ready")
        row_ready = sem("row_ready")
        rowu_ready = sem("rowu_ready")
        gate_ready = sem("gate_ready")
        id_ready = sem("id_ready")
        entries_stored = sems("entries_stored", TOP_K * NT)

        plan = sem("plan")
        tablerow_ready = sem("tablerow_ready")
        experts_ready = sem("experts_ready")
        byslot1_loaded = sem("byslot1_loaded")
        byslot2_loaded = sem("byslot2_loaded")
        byslot_done = sem("byslot_done")
        ids_ready = sem("ids_ready")
        gates_ready = sem("gates_ready")

        gid_ready = sem("gid_ready")
        sid_ready = sem("sid_ready")
        xg_loaded = sems("xg_loaded", 2)
        xgt_done = sem("xgt_done")
        xgthi_ready = sem("xgthi_ready")
        xgtlo_ready = sem("xgtlo_ready")
        up1_done = sem("up1_done")
        up3_done = sem("up3_done")
        silu_ready = sem("silu_ready")
        h_ready = sem("h_ready")
        ht_done = sem("ht_done")
        hthi_ready = sem("hthi_ready")
        htlo_ready = sem("htlo_ready")
        down_done = sem("down_done")
        y_ready = sem("y_ready")
        y_added = sem("y_added")

        xnt_ps = bank[0][:, :].rearrange("p (c n) -> p c n", c=DC)
        g_ps = bank[1][:, :].rearrange("p (c n) -> p c n", c=DC)
        v_ps = bank[2][:, :].rearrange("p (t n) -> p t n", t=NT)
        rel_ps = bank[3][:, :].rearrange("p (t n) -> p t n", t=NT)
        mix_ps = bank[4][:, :].rearrange("p (t n) -> p t n", t=NT)
        xn2t_ps = bank[5][:, :].rearrange("p (c n) -> p c n", c=DC)
        norm_ps = bank[6][:, 0:NT]
        RE = NT * EXPERTS
        logit_ps = bank[7][:, 0:RE].rearrange("p (t e) -> p t e", t=NT)
        rank_ps = bank[6][:, 64:64 + RE].rearrange("p (t e) -> p t e", t=NT)
        count_ps = bank[6][:, 64 + RE:64 + RE + EXPERTS]
        byslot1_ps = bank[7][:, 128:128 + 2 * P].rearrange("p (c s) -> p c s", c=2)
        byslot2_ps = bank[6][:, 128:128 + 2 * S2].rearrange("p (c s) -> p c s", c=2)
        up1_ps, up3_ps = bank[0], bank[1]
        ht_ps = bank[2][:, :].rearrange("p (c n) -> p c n", c=HC)
        xgt_ps = bank[3][:, 0:DC * P].rearrange("p (c n) -> p c n", c=DC)
        down_ps = bank[4][:, 0:D]

        x_rows = x.rearrange("b (t p) d -> (b t) p d", p=P)
        out_rows = out.rearrange("(r p) d -> r p d", p=P)
        token_rows = tokens_dram.rearrange("(r p) d -> r p d", p=P)

        def batch_rows(rows, b):
            return rows[bass.ds(b.value(NT), NT), :, :].rearrange("t p d -> p t d")

        LAG = 6
        G_ROLL = (LAG + 2, LAG + 1 + (BATCHES - LAG - 3) // UNROLL * UNROLL)
        pieces = {}
        for n in range(2 * EXPERTS):
            k = 2 + n // 2 if n < 2 * EXPERTS - 4 else G_ROLL[1] + 1 + n - (2 * EXPERTS - 4)
            pieces.setdefault(k, []).append(n)
        assert not any(G_ROLL[0] <= k <= G_ROLL[1] for k in pieces)

        def up_piece(n, *of):
            e, which = n // 2, n % 2
            return [pair[which][:, e * DC * HID:(e + 1) * DC * HID] for pair in of]

        def down_piece(e, *of):
            return [t[:, e * HC * D:(e + 1) * HC * D] for t in of]

        def graph_steps(eng, body):
            steps(eng, 0, BATCHES - 1 + LAG, *G_ROLL, UNROLL, body)

        E_ROLL = (3, 3 + (SLOTS - 4) // UNROLL * UNROLL - 1)

        def expert_steps(eng, body):
            steps(eng, 0, SLOTS, *E_ROLL, UNROLL, body)

        block = ctx.enter_context(nc.Block())

        @block.sync
        def _(sp):
            def load_x(b):
                sp.dma_start(x_in[:, b.place(XR)], batch_rows(x_rows, b)).then_inc(x_loaded[b.place(XR)], 16)

            load_x(Index(0))
            for w, to in ((w_q, wq_sb), (w_k, wk_sb), (w_v, wv_sb)):
                sp.dma_start(to[:, :, :], w.rearrange("(c p) d -> p c d", p=P)).then_inc(graph_w_loaded, 16)
            sp.dma_start(adj_sb[:, :, :], adj.rearrange("(t p) n -> p t n", p=P)).then_inc(adj_loaded, 16)
            for b in range(1, XR):
                load_x(Index(b))
            sp.dma_start(wg_sb[:, :, :], w_gate.rearrange("(c p) e -> p c e", p=P)).then_inc(gate_w_loaded, 16)
            sp.dma_start(bg_sb[:, :], b_gate.partition_broadcast(P)).then_inc(gate_w_loaded, 16)
            sp.wait_ge(zeros_made, 1)
            sp.dma_start(token_rows[TILES], zero_rows[:, :]).then_inc(spare_stored, 16)
            sp.dma_start(out_rows[TILES], zero_rows[:, :]).then_inc(spare_stored, 16)
            sp.wait_ge(blank_made, 1)
            for table in tables:
                sp.dma_start(table.rearrange("(p j) c -> p j c", p=P), blank[:, :, :]).then_inc(blank_stored, 16)

            def step(k):
                b = k - 3
                if b.within(BATCHES):
                    wait(sp, x1_ready, b.value(NT, NT))
                    sp.dma_start(batch_rows(out_rows, b), x1[:, b.place(2)]).then_inc(x1_stored[b.place(2)], 16)
                nxt = k + 1
                if nxt.within(BATCHES) and (nxt.i is not None or nxt.base >= XR):
                    load_x(nxt)
                if b.within(BATCHES):
                    wait(sp, xn2_ready, b.value(NT, NT))
                    sp.dma_start(batch_rows(token_rows, b), xn2[:, b.place(2)]).then_inc(xn2_stored[b.place(2)], 16)

            graph_steps(sp, step)

            for q in range(2):
                sp.wait_ge(x1_stored[q], BATCHES // 2 * 16)
                sp.wait_ge(xn2_stored[q], BATCHES // 2 * 16)
            for e in range(EXPERTS):
                if e == EXPERTS - 1:
                    sp.wait_ge(rowu_ready, BATCHES)
                    sp.wait_ge(id_ready, BATCHES * TOP_K)
                    sp.wait_ge(gate_ready, BATCHES * TOP_K)
                (to,) = down_piece(e, w2_raw)
                sp.dma_start(to.rearrange("p (c n) -> p c n", c=HC),
                             w_2[e].rearrange("(c p) n -> p c n", p=P)).then_inc(down_loaded[e], 16)

        @block.gpsimd
        def _(pool):
            pool.memset(ident[:, :], 0.0).then_inc(ident_zero, 1)
            pool.memset(before[:, :], 1.0).then_inc(ident_zero, 1)
            pool.wait_ge(ident_zero, 2)
            pool.affine_select(out=ident[:, :], in_=ident[:, :], compare_op=ALU.not_equal, fill=1.0, base=0,
                               pattern=[[-1, P]], channel_multiplier=1).then_inc(ident_made, 1)
            pool.affine_select(out=before[:, :], in_=before[:, :], compare_op=ALU.is_gt, fill=0.0, base=0,
                               pattern=[[1, P]], channel_multiplier=-1).then_inc(before_made, 1)
            pool.memset(zero_rows[:, :], 0.0).then_inc(zeros_made, 1)
            pool.memset(half[:, :], -0.5).then_inc(iotas_made, 1)
            pool.iota(expert_no[:, :], [[1, EXPERTS]], base=0, channel_multiplier=0,
                      allow_small_or_imprecise_dtypes=True).then_inc(iotas_made, 1)
            pool.iota(start_row[:, :], [[TOKENS, EXPERTS]], base=-SPARE, channel_multiplier=-1,
                      allow_small_or_imprecise_dtypes=True).then_inc(iotas_made, 1)
            pool.iota(spare_row[:, :], [[0, 1]], base=SPARE, channel_multiplier=1,
                      allow_small_or_imprecise_dtypes=True).then_inc(iotas_made, 1)
            pool.iota(token_no[:, :], [[P, TILES]], base=1, channel_multiplier=1,
                      allow_small_or_imprecise_dtypes=True).then_inc(iotas_made, 1)
            pool.iota(slot_no[:, :], [[P, 2]], base=0, channel_multiplier=1,
                      allow_small_or_imprecise_dtypes=True).then_inc(iotas_made, 1)
            pool.iota(slot_free[:, :], [[1, SLOTS]], base=0, channel_multiplier=0,
                      allow_small_or_imprecise_dtypes=True).then_inc(iotas_made, 1)
            pool.iota(pad_id[:, :], [[0, 1]], base=TOKENS + 1, channel_multiplier=1,
                      allow_small_or_imprecise_dtypes=True).then_inc(iotas_made, 1)

            def store_entries(c, kk):
                q = c.place(2)
                for t in range(NT):
                    j = kk * NT + t
                    wait(pool, entries_stored[j], c.value(16))
                    hold(pool, held_pool)
                    pool.indirect_dma_start(
                        tables[j][:, :], bass.IndirectOffsetOnAxis(row_u[:, q, j:j + 1], 0),
                        entry[:, q, kk, t, :], None).then_inc(entries_stored[j], 16)

            def step(k):
                r = k - 5
                if r.within(BATCHES):
                    for stored in entries_stored:
                        wait(pool, stored, (r - 1).value(16))
                    for kk in range(TOP_K):
                        pool.tensor_copy(entry[:, r.place(2), kk, :, 0], token_no[:, bass.ds(r.value(NT), NT)]) \
                            .then_inc(id_ready, 1)
                b = k - 3
                if b.within(BATCHES):
                    wait(pool, normsq_ready, b.value(1, 1))
                    wait(pool, x1_ready, b.value(NT))
                    pool.tensor_tensor(norm_inv[:, :], norm_sq[:, :], half[:, :], ALU.pow).then_inc(norminv_ready, 1)
                c = k - 6
                if c.within(BATCHES):
                    wait(pool, id_ready, c.value(TOP_K, TOP_K))
                    wait(pool, gate_ready, c.value(TOP_K, TOP_K))
                    wait(pool, rowu_ready, c.value(1, 1))
                    if c.i is None and c.base == 0:
                        pool.wait_ge(blank_stored, 16 * len(tables))
                    store_entries(c, 0)
                if b.within(BATCHES):
                    wait(pool, var2_ready, b.value(1, 1))
                    wait(pool, xn2_ready, b.value(NT))
                    pool.tensor_tensor(rstd2[:, :], var2[:, :], half[:, :], ALU.pow).then_inc(rstd2_ready, 1)
                if k.within(BATCHES):
                    if k.i is None and k.base == 0:
                        pool.wait_ge(iotas_made, 8)
                    wait(pool, var1_ready, k.value(1, 1))
                    wait(pool, xn_ready, (k - 1).value(NT))
                    pool.tensor_tensor(rstd1[:, k.place(2)], var1[:, k.place(2)], half[:, :],
                                       ALU.pow).then_inc(rstd1_ready, 1)
                if c.within(BATCHES):
                    store_entries(c, 1)

            graph_steps(pool, step)

            pool.wait_ge(tablerow_ready, 1)
            pool.wait_ge(blank_stored, 16 * len(tables))
            for n, to, loaded in ((P, by_slot1, byslot1_loaded), (S2, by_slot2, byslot2_loaded)):
                at = table_row_u[0:n, 0:1] if n == P else table_row_u[0:n, 1:2]
                for j, table in enumerate(tables):
                    pool.wait_ge(entries_stored[j], 16 * BATCHES)
                    pool.indirect_dma_start(to[:, j].rearrange("s p c -> s (p c)"), None,
                                            table.rearrange("(r p) c -> r (p c)", p=P),
                                            bass.IndirectOffsetOnAxis(at, 0)).then_inc(loaded, 16)
            for q in range(2):
                pool.wait_ge(xn2_stored[q], BATCHES // 2 * 16)
                pool.wait_ge(x1_stored[q], BATCHES // 2 * 16)
            pool.wait_ge(spare_stored, 32)
            pool.wait_ge(ids_ready, 1)
            pool.wait_ge(byslot_done, 2)

            def gather(s):
                q = s.place(2)
                wait(pool, xgt_done, (s - 1).value())
                pool.tensor_copy(gather_id[:, q:q + 1], ids[:, bass.ds(s.value(), 1)]).then_inc(gid_ready, 1)
                wait(pool, gid_ready, s.value(1, 1))
                hold(pool, held_pool)
                pool.indirect_dma_start(xg[:, q, :], None, tokens_dram[:, :],
                                        bass.IndirectOffsetOnAxis(gather_id[:, q:q + 1], 0)) \
                    .then_inc(xg_loaded[q], 16)

            def add(s):
                q = s.place(2)
                wait(pool, y_added, (s - 1).value(16))
                pool.tensor_copy(scatter_id[:, q:q + 1], ids[:, bass.ds(s.value(), 1)]).then_inc(sid_ready, 1)
                wait(pool, sid_ready, s.value(1, 1))
                wait(pool, y_added, s.value(16))
                wait(pool, y_ready, s.value(1, 1))
                hold(pool, held_pool)
                pool.indirect_dma_start(out[:, :], bass.IndirectOffsetOnAxis(scatter_id[:, q:q + 1], 0),
                                        y[:, q, :], None, compute_op=ALU.add).then_inc(y_added, 16)

            gather(Index(0))
            gather(Index(1))
            pool.wait_ge(ids_ready, 2)

            def expert_step(s):
                if (s + 2).within(SLOTS):
                    gather(s + 2)
                if (s - 1).within(SLOTS):
                    add(s - 1)

            steps(pool, 0, SLOTS, 3, 3 + (SLOTS - 4) // 2 * 2 - 1, 2, expert_step)
            pool.wait_ge(y_added, 16 * SLOTS)

        @block.scalar
        def _(act):
            for n in range(2 * EXPERTS):
                (to,) = up_piece(n, (w1_raw, w3_raw))
                act.dma_start(to.rearrange("p (c n) -> p c n", c=DC),
                              (w_1, w_3)[n % 2][n // 2].rearrange("(c p) n -> p c n", p=P)) \
                    .then_inc(up_loaded[n], 16)
            act.wait_ge(a_done, 1)
            act.copy(at_hi[:, :, :], g_ps).then_inc(a_hi_ready, 1)
            act.wait_ge(wvt_done, 1)
            act.copy(wvt_hi[:, :, :], v_ps).then_inc(wvt_hi_ready, 1)

            def step(k):
                b = k - 1
                if b.within(BATCHES):
                    q = b.place(2)
                    wait(act, xnt_done, b.value(1, 1))
                    wait(act, rel_done, (b - 1).value())
                    act.copy(xn_t[:, q], xnt_ps).then_inc(xnt_ready, 1)
                    wait(act, xnt_ready, b.value(1, 1))
                    act.copy(xnt_hi[:, q], xn_t[:, q]).then_inc(xnthi_ready, 1)
                m = k - 2
                if m.within(BATCHES):
                    wait(act, g_done, m.value(1, 1))
                    wait(act, rel_done, m.value())
                    act.copy(g_t[:, :, :], g_ps).then_inc(g_ready, 1)
                    wait(act, v_done, m.value(1, 1))
                    wait(act, mix_done, m.value())
                    act.copy(v[:, :, :], v_ps).then_inc(v_ready, 1)
                b = k - 4
                if b.within(BATCHES):
                    wait(act, xn2t_done, b.value(1, 1))
                    wait(act, logit_done, b.value())
                    act.copy(xn2_t[:, :, :], xn2t_ps).then_inc(xn2t_ready, 1)
                if k.i is None:
                    for n in pieces.get(k.base, []):
                        hi, raw = up_piece(n, (w1_hi, w3_hi), (w1_raw, w3_raw))
                        act.wait_ge(up_loaded[n], 16)
                        act.copy(hi, raw).then_inc(up_hi_ready, 1)
                r = k - 5
                if r.within(BATCHES):
                    wait(act, margin_ready, r.value(1, 1))
                    wait(act, id_ready, r.value(TOP_K, TOP_K))
                    for kk, sign in ((0, 1.0), (1, -1.0)):
                        act.activation(entry[:, r.place(2), kk, :, 1], margin[:, :], ACT.Sigmoid,
                                       scale=sign).then_inc(gate_ready, 1)
                if m.within(BATCHES):
                    wait(act, rel_ready, m.value(1, 1))
                    wait(act, norm_done, m.value())
                    act.activation(rel_sq[:, :, :], rel[:, :, :], ACT.Square).then_inc(relsq_ready, 1)
                if k.within(BATCHES):
                    q = k.place(2)
                    wait(act, shift1_ready, k.value(1, 1))
                    wait(act, xnt_done, (k - 1).value())
                    for t in range(NT):
                        act.activation(xn[:, q, t, :], x_in[:, k.place(XR), t, :], ACT.Identity,
                                       bias=shift1[:, q, t:t + 1], scale=rstd1[:, q, t:t + 1]).then_inc(xn_ready, 1)

            graph_steps(act, step)

            def down_hi(e):
                hi, raw = down_piece(e, w2_hi, w2_raw)
                act.wait_ge(down_loaded[e], 16)
                if e == 0:
                    act.wait_ge(x1_ready, BATCHES * NT)
                if e == EXPERTS - 1:
                    act.wait_ge(xn2t_done, BATCHES)
                act.copy(hi, raw).then_inc(down_hi_ready, 1)

            for e in range(EXPERTS):
                down_hi(e)
            act.wait_ge(byslot_done, 1)
            act.copy(gates[:, 0:P], byslot1_ps[:, 1, :]).then_inc(gates_ready, 1)

            def transposed(s):
                wait(act, xgt_done, s.value(1, 1))
                act.copy(xgt_hi[:, :, :], xgt_ps).then_inc(xgthi_ready, 1)

            act.wait_ge(byslot_done, 2)
            act.copy(gates[:, P:SLOTS], byslot2_ps[:, 1, :]).then_inc(gates_ready, 1)
            act.wait_ge(gates_ready, 2)
            transposed(Index(0))

            def expert_step(s):
                d = s - 1
                if d.within(SLOTS):
                    wait(act, ht_done, d.value(1, 1))
                    wait(act, down_done, d.value())
                    act.copy(ht_hi[:, :, :], ht_ps).then_inc(hthi_ready, 1)
                if s.within(SLOTS):
                    wait(act, up1_done, s.value(1, 1))
                    wait(act, ht_done, s.value())
                    act.activation(h[:, :], up1_ps[:, :], ACT.Silu).then_inc(silu_ready, 1)
                if (s + 1).within(SLOTS):
                    transposed(s + 1)
                if d.within(SLOTS):
                    wait(act, down_done, d.value(1, 1))
                    wait(act, y_added, (d - 1).value(16))
                    act.activation(y[:, d.place(2), :], down_ps, ACT.Copy,
                                   scale=gates[:, bass.ds(d.value(), 1)]).then_inc(y_ready, 1)

            expert_steps(act, expert_step)

        @block.vector
        def _(dve):
            dve.memset(ones[:, :], 1.0).then_inc(consts_made, 1)
            dve.memset(ones_col[:, :], 1.0).then_inc(consts_made, 1)
            dve.memset(all_ones[:, :], 1.0).then_inc(consts_made, 1)
            dve.memset(blank[:, :, :], 0.0).then_inc(blank_made, 1)
            dve.wait_ge(iotas_made, 8)
            dve.tensor_copy(first_free[:, :], start_row[:, :]).then_inc(free_ready, 1)
            dve.wait_ge(a_hi_ready, 1)
            dve.tensor_tensor(at_lo[:, :, :], g_ps, at_hi[:, :, :], ALU.subtract).then_inc(a_lo_ready, 1)
            dve.wait_ge(wvt_hi_ready, 1)
            dve.tensor_tensor(wvt_lo[:, :, :], v_ps, wvt_hi[:, :, :], ALU.subtract).then_inc(wvt_lo_ready, 1)

            split = {n: i + 1 for i, n in enumerate(n for k in sorted(pieces) for n in pieces[k])}

            def split_up(n):
                hi, lo, raw = up_piece(n, (w1_hi, w3_hi), (w1_lo, w3_lo), (w1_raw, w3_raw))
                dve.wait_ge(up_hi_ready, split[n])
                dve.tensor_tensor(lo, raw, hi, ALU.subtract).then_inc(up_lo_ready, 1)
            def step(k):
                b = k - 3
                if b.within(BATCHES):
                    wait(dve, norm_done, b.value(1, 1))
                    wait(dve, norminv_ready, b.value())
                    dve.tensor_copy(norm_sq[:, :], norm_ps).then_inc(normsq_ready, 1)
                r = k - 5
                if r.within(BATCHES):
                    if r.i is None and r.base == 0:
                        dve.wait_ge(gate_w_loaded, 32)
                    wait(dve, logit_done, r.value(1, 1))
                    dve.tensor_tensor(logit[:, :, :], logit_ps,
                                      bg_sb[:, :].unsqueeze(1).to_broadcast([P, NT, EXPERTS]),
                                      ALU.add).then_inc(logit_ready, 1)
                    wait(dve, logit_ready, r.value(1, 1))
                    hold(dve, held_dve)
                    for t in range(NT):
                        dve.max(top[:, t, :], logit[:, t, :]).then_inc(top_ready, 1)
                    wait(dve, top_ready, r.value(NT, NT))
                    hold(dve, held_dve)
                    for t in range(NT):
                        dve.max_index(top_at[:, t, :], top[:, t, :], logit[:, t, :]).then_inc(topat_ready, 1)
                    wait(dve, gate_ready, r.value(TOP_K))
                    dve.tensor_tensor(margin[:, :], top[:, :, 0], top[:, :, 1], ALU.subtract) \
                        .then_inc(margin_ready, 1)
                    wait(dve, topat_ready, r.value(NT, NT))
                    dve.tensor_copy(top_no[:, :, :], top_at[:, :, 0:TOP_K].rearrange("p t k -> p k t")) \
                        .then_inc(topno_ready, 1)
                    wait(dve, topno_ready, r.value(1, 1))
                    for kk in range(TOP_K):
                        dve.tensor_tensor(chosen[:, kk], expert_no[:, :].unsqueeze(1).to_broadcast([P, NT, EXPERTS]),
                                          top_no[:, kk, :].unsqueeze(2).to_broadcast([P, NT, EXPERTS]),
                                          ALU.is_equal).then_inc(chosen_ready, 1)
                    wait(dve, chosen_ready, r.value(TOP_K, TOP_K))
                    wait(dve, prefix_done, r.value())
                    dve.tensor_tensor(either[:, :, :], chosen[:, 0], chosen[:, 1], ALU.add).then_inc(either_ready, 1)
                t_ = k - 1
                if t_.within(BATCHES):
                    q = t_.place(2)
                    wait(dve, xnthi_ready, t_.value(1, 1))
                    wait(dve, v_done, (t_ - 1).value())
                    dve.tensor_tensor(xnt_lo[:, q], xn_t[:, q], xnt_hi[:, q], ALU.subtract).then_inc(xntlo_ready, 1)
                b = k - 3
                if b.within(BATCHES):
                    q = b.place(2)
                    wait(dve, norminv_ready, b.value(1, 1))
                    wait(dve, mix_done, b.value(1, 1))
                    wait(dve, x1_stored[q], b.before(2) * 16)
                    for t in range(NT):
                        dve.scalar_tensor_tensor(x1[:, q, t, :], mix_ps[:, t, :], norm_inv[:, t:t + 1],
                                                 x_in[:, b.place(XR), t, :], ALU.mult, ALU.add) \
                            .then_inc(x1_ready, 1)
                    wait(dve, x1_ready, b.value(NT, NT))
                    for t in range(NT):
                        dve.bn_stats(part2[:, t, :], x1[:, q, t, :]).then_inc(part2_ready, 1)
                    wait(dve, part2_ready, b.value(NT, NT))
                    hold(dve, held_dve)
                    for t in range(NT):
                        dve.bn_aggr(mean2[:, t, :], part2[:, t, :]).then_inc(mean2_ready, 1)
                    wait(dve, mean2_ready, b.value(NT, NT))
                    wait(dve, rstd2_ready, b.value())
                    dve.tensor_scalar(var2[:, :], mean2[:, :, 1], EPS, None, ALU.add).then_inc(var2_ready, 1)
                if k.within(BATCHES):
                    q = k.place(2)
                    wait(dve, x_loaded[k.place(XR)], k.before(XR) * 16 + 16)
                    for t in range(NT):
                        dve.bn_stats(part1[:, t, :], x_in[:, k.place(XR), t, :]).then_inc(part1_ready, 1)
                    wait(dve, part1_ready, k.value(NT, NT))
                    hold(dve, held_dve)
                    for t in range(NT):
                        dve.bn_aggr(mean1[:, q, t, :], part1[:, t, :]).then_inc(mean1_ready, 1)
                    wait(dve, mean1_ready, k.value(NT, NT))
                    wait(dve, shift1_ready, (k - 1).value())
                    dve.tensor_scalar(var1[:, q, :], mean1[:, q, :, 1], EPS, None, ALU.add).then_inc(var1_ready, 1)
                m = k - 2
                if m.within(BATCHES):
                    if m.i is None and m.base == 0:
                        dve.wait_ge(adj_loaded, 16)
                    wait(dve, rel_done, m.value(1, 1))
                    wait(dve, mix_done, m.value())
                    wait(dve, relsq_ready, m.value())
                    dve.tensor_tensor(rel[:, :, :], rel_ps, adj_sb[:, :, :], ALU.mult).then_inc(rel_ready, 1)
                if r.within(BATCHES):
                    wait(dve, prefix_done, r.value(1, 1))
                    wait(dve, free_ready, r.value(1, 1))
                    dve.tensor_tensor(rank[:, :, :], rank_ps,
                                      first_free[:, :].unsqueeze(1).to_broadcast([P, NT, EXPERTS]),
                                      ALU.add).then_inc(rank_ready, 1)
                    wait(dve, rank_ready, r.value(1, 1))
                    dve.tensor_tensor(first_free[:, :], count_ps, first_free[:, :], ALU.add).then_inc(free_ready, 1)
                    for kk in range(TOP_K):
                        dve.tensor_tensor(picked[:, kk * NT:(kk + 1) * NT, :], chosen[:, kk], rank[:, :, :],
                                          ALU.mult).then_inc(picked_ready, 1)
                    wait(dve, picked_ready, r.value(TOP_K, TOP_K))
                    dve.tensor_reduce(row[:, :], picked[:, :, :], AX_X, ALU.add).then_inc(row_ready, 1)
                    wait(dve, row_ready, r.value(1, 1))
                    wait(dve, id_ready, r.value(TOP_K, TOP_K))
                    dve.tensor_scalar(row_u[:, r.place(2), :], row[:, :], spare_row[:, 0:1], None,
                                      ALU.add).then_inc(rowu_ready, 1)
                if b.within(BATCHES):
                    q = b.place(2)
                    wait(dve, rstd2_ready, b.value(1, 1))
                    wait(dve, xn2_stored[q], b.before(2) * 16)
                    wait(dve, xn2t_done, (b - 1).value())
                    for t in range(NT):
                        dve.tensor_scalar(xn2[:, q, t, :], x1[:, q, t, :], mean2[:, t, 0:1], rstd2[:, t:t + 1],
                                          ALU.subtract, ALU.mult).then_inc(xn2_ready, 1)
                if k.within(BATCHES):
                    q = k.place(2)
                    wait(dve, rstd1_ready, k.value(1, 1))
                    dve.scalar_tensor_tensor(shift1[:, q, :], mean1[:, q, :, 0], -1.0, rstd1[:, q, :],
                                             ALU.mult, ALU.mult).then_inc(shift1_ready, 1)
                if k.i is None:
                    for n in pieces.get(k.base, []):
                        split_up(n)

            graph_steps(dve, step)

            n = 0
            dve.wait_ge(free_ready, BATCHES + 1)
            dve.tensor_tensor(count_i[:, :], first_free[:, :], start_row[:, :], ALU.subtract).then_inc(plan, 1)
            dve.wait_ge(plan, n + 1)
            dve.tensor_scalar(count_i[:, :], count_i[:, :], P - 1, None, ALU.add).then_inc(plan, 1)
            dve.wait_ge(plan, n + 2)
            dve.tensor_scalar(slots_i[:, :], count_i[:, :], P.bit_length() - 1, None,
                              ALU.logical_shift_right).then_inc(plan, 1)
            dve.wait_ge(plan, n + 3)
            dve.tensor_copy(slots_of[:, :], slots_i[:, :]).then_inc(plan, 1)
            dve.wait_ge(plan, n + 4)
            dve.tensor_tensor_scan(slots_end[:, :], all_ones[:, :], slots_of[:, :], 0.0, ALU.mult, ALU.add) \
                .then_inc(plan, 1)
            dve.tensor_scalar(slot_gap[:, :], slots_of[:, :], -1.0, float(TILES), ALU.mult, ALU.add).then_inc(plan, 1)
            dve.wait_ge(plan, n + 6)
            for j in range(2):
                dve.tensor_scalar(past[:, j, :], slots_end[:, :], slot_no[:, j:j + 1], None, ALU.is_le) \
                    .then_inc(plan, 1)
            dve.wait_ge(plan, n + 8)
            dve.tensor_tensor(skipped[:, :, :], past[:, :, :],
                              slot_gap[:, :].unsqueeze(1).to_broadcast([P, 2, EXPERTS]), ALU.mult).then_inc(plan, 1)
            dve.wait_ge(plan, n + 9)
            dve.tensor_reduce(table_row[:, :], skipped[:, :, :], AX_X, ALU.add).then_inc(plan, 1)
            dve.wait_ge(plan, n + 10)
            dve.tensor_tensor(table_row_u[:, :], table_row[:, :], slot_no[:, :], ALU.add).then_inc(tablerow_ready, 1)
            dve.tensor_scalar(expert_f[:, :], slot_free[:, :], slots_end[0:1, 0:1], None, ALU.is_ge) \
                .then_inc(plan, 1)
            for e in range(1, EXPERTS):
                dve.wait_ge(plan, n + 10 + e)
                dve.scalar_tensor_tensor(expert_f[:, :], slot_free[:, :], slots_end[0:1, e:e + 1], expert_f[:, :],
                                         ALU.is_ge, ALU.add).then_inc(plan, 1)
            n += 10 + EXPERTS
            dve.wait_ge(plan, n)
            dve.tensor_scalar(weights_at[:, :], expert_f[:, :], float(EXPERTS - 1), float(WEIGHTS), ALU.min, ALU.mult) \
                .then_inc(experts_ready, 1)
            for e in range(EXPERTS):
                hi, lo, raw = down_piece(e, w2_hi, w2_lo, w2_raw)
                dve.wait_ge(down_hi_ready, e + 1)
                dve.tensor_tensor(lo, raw, hi, ALU.subtract).then_inc(down_lo_ready, 1)

            def name_tokens(c, ps, at):
                dve.wait_ge(byslot_done, c + 1)
                dve.wait_ge(gates_ready, c + 1)
                dve.tensor_copy(id_sum[:, at], ps[:, 0, :]).then_inc(plan, 1)
                dve.wait_ge(plan, n + 2 * c + 1)
                dve.tensor_scalar(is_pad[:, at], id_sum[:, at], 0.0, pad_id[:, 0:1], ALU.is_equal, ALU.mult) \
                    .then_inc(plan, 1)
                dve.wait_ge(plan, n + 2 * c + 2)
                dve.scalar_tensor_tensor(ids[:, at], id_sum[:, at], -1.0, is_pad[:, at], ALU.add, ALU.add) \
                    .then_inc(ids_ready, 1)

            name_tokens(0, byslot1_ps, slice(0, P))
            name_tokens(1, byslot2_ps, slice(P, SLOTS))
            dve.wait_ge(ids_ready, 2)

            def transposed(s):
                wait(dve, xgthi_ready, s.value(1, 1))
                dve.tensor_tensor(xgt_lo[:, :, :], xgt_ps, xgt_hi[:, :, :], ALU.subtract).then_inc(xgtlo_ready, 1)

            transposed(Index(0))

            def expert_step(s):
                d = s - 1
                if d.within(SLOTS):
                    wait(dve, hthi_ready, d.value(1, 1))
                    dve.tensor_tensor(ht_lo[:, :, :], ht_ps, ht_hi[:, :, :], ALU.subtract).then_inc(htlo_ready, 1)
                if s.within(SLOTS):
                    wait(dve, up3_done, s.value(1, 1))
                    wait(dve, silu_ready, s.value(1, 1))
                    dve.tensor_tensor(h[:, :], up3_ps[:, :], h[:, :], ALU.mult).then_inc(h_ready, 1)
                if (s + 1).within(SLOTS):
                    transposed(s + 1)

            expert_steps(dve, expert_step)

        @block.tensor
        def _(pe):
            def product(out_ps, left, right, first, last):
                for i, (a, b) in enumerate(((0, 0), (0, 1), (1, 0))):
                    mm = pe.matmul(out_ps, left[a], right[b], start=(first and i == 0), stop=(last and i == 2))
                return mm

            pe.wait_ge(ident_made, 1)
            pe.wait_ge(graph_w_loaded, 48)
            for c in range(DC):
                for e in range(DC):
                    mm = pe.matmul(g_ps[:, c, :], wq_sb[:, e, c * P:(c + 1) * P], wk_sb[:, e, :],
                                   start=(e == 0), stop=(e == DC - 1))
            mm.then_inc(a_done, 1)
            for c in range(DC):
                for e in range(DC):
                    mm = pe.transpose(v_ps[:, c, e * P:(e + 1) * P], wv_sb[:, e, c * P:(c + 1) * P], ident[:, :])
            mm.then_inc(wvt_done, 1)

            def step(k):
                b = k - 1
                if b.within(BATCHES):
                    wait(pe, xn_ready, b.value(NT, NT))
                    wait(pe, xnt_ready, b.value())
                    for t in range(NT):
                        for c in range(DC):
                            mm = pe.transpose(xnt_ps[:, c, t * P:(t + 1) * P],
                                              xn[:, b.place(2), t, c * P:(c + 1) * P], ident[:, :])
                    mm.then_inc(xnt_done, 1)
                m = k - 2
                if m.within(BATCHES):
                    q = m.place(2)
                    xt = xn_t[:, q]
                    if m.i is None and m.base == 0:
                        pe.wait_ge(a_hi_ready, 1)
                        pe.wait_ge(a_lo_ready, 1)
                        pe.wait_ge(wvt_hi_ready, 1)
                        pe.wait_ge(wvt_lo_ready, 1)
                    wait(pe, xntlo_ready, m.value(1, 1))
                    wait(pe, g_ready, m.value())
                    for c in range(DC):
                        cols = slice(c * P, (c + 1) * P)
                        for e in range(DC):
                            mm = product(g_ps[:, c, :], (at_hi[:, e, cols], at_lo[:, e, cols]),
                                         (xnt_hi[:, q, e, :], xnt_lo[:, q, e, :]), e == 0, e == DC - 1)
                    mm.then_inc(g_done, 1)
                    wait(pe, v_ready, m.value())
                    for t in range(NT):
                        for e in range(DC):
                            cols = slice(t * P, (t + 1) * P)
                            mm = product(v_ps[:, t, :], (xnt_hi[:, q, e, cols], xnt_lo[:, q, e, cols]),
                                         (wvt_hi[:, e, :], wvt_lo[:, e, :]), e == 0, e == DC - 1)
                    mm.then_inc(v_done, 1)
                r = k - 5
                if r.within(BATCHES):
                    if r.i is None and r.base == 0:
                        pe.wait_ge(before_made, 1)
                        pe.wait_ge(consts_made, 2)
                    wait(pe, either_ready, r.value(1, 1))
                    pe.matmul(rank_ps[:, 0, :], before[:, :], either[:, 0, :], start=True, stop=True)
                    pe.matmul(rank_ps[:, 1, :], before[:, :], either[:, 1, :], start=True, stop=False)
                    pe.matmul(rank_ps[:, 1, :], ones[:, :], either[:, 0, :], start=False, stop=True)
                    pe.matmul(count_ps, ones[:, :], either[:, 0, :], start=True, stop=False)
                    pe.matmul(count_ps, ones[:, :], either[:, 1, :], start=False, stop=True).then_inc(prefix_done, 1)
                b = k - 4
                if b.within(BATCHES):
                    wait(pe, xn2_ready, b.value(NT, NT))
                    wait(pe, xn2t_ready, b.value())
                    for t in range(NT):
                        for c in range(DC):
                            mm = pe.transpose(xn2t_ps[:, c, t * P:(t + 1) * P],
                                              xn2[:, b.place(2), t, c * P:(c + 1) * P], ident[:, :])
                    mm.then_inc(xn2t_done, 1)
                if m.within(BATCHES):
                    wait(pe, g_ready, m.value(1, 1))
                    wait(pe, rel_ready, m.value())
                    for t in range(NT):
                        for e in range(DC):
                            mm = pe.matmul(rel_ps[:, t, :], xt[:, e, t * P:(t + 1) * P], g_t[:, e, :],
                                           start=(e == 0), stop=(e == DC - 1))
                    mm.then_inc(rel_done, 1)
                if b.within(BATCHES):
                    if b.i is None and b.base == 0:
                        pe.wait_ge(gate_w_loaded, 32)
                    wait(pe, xn2t_ready, b.value(1, 1))
                    wait(pe, logit_ready, b.value())
                    for t in range(NT):
                        for e in range(DC):
                            mm = pe.matmul(logit_ps[:, t, :], xn2_t[:, e, t * P:(t + 1) * P], wg_sb[:, e, :],
                                           start=(e == 0), stop=(e == DC - 1))
                    mm.then_inc(logit_done, 1)
                if m.within(BATCHES):
                    wait(pe, rel_ready, m.value(1, 1))
                    wait(pe, v_ready, m.value(1, 1))
                    wait(pe, x1_ready, m.value(NT))
                    for t in range(NT):
                        for e in range(NT):
                            mm = pe.matmul(mix_ps[:, t, :], rel[:, e, t * P:(t + 1) * P], v[:, e, :],
                                           start=(e == 0), stop=(e == NT - 1))
                    mm.then_inc(mix_done, 1)
                    wait(pe, relsq_ready, m.value(1, 1))
                    wait(pe, normsq_ready, m.value())
                    if r.within(BATCHES):
                        wait(pe, free_ready, r.value(1, 2))
                    for t in range(NT):
                        for e in range(NT):
                            mm = pe.matmul(norm_ps[:, t:t + 1], rel_sq[:, e, t * P:(t + 1) * P], ones_col[:, :],
                                           start=(e == 0), stop=(e == NT - 1))
                    mm.then_inc(norm_done, 1)

            graph_steps(pe, step)

            def by_row(n, of, ps):
                for c in range(2):
                    for j in range(len(tables)):
                        mm = pe.matmul(ps[:, c, :], of[:, j, :, c], ident[0:n, 0:n],
                                       start=(j == 0), stop=(j == len(tables) - 1))
                mm.then_inc(byslot_done, 1)

            pe.wait_ge(byslot1_loaded, 16 * len(tables))
            pe.wait_ge(rank_ready, BATCHES)
            pe.wait_ge(free_ready, BATCHES + 1)
            by_row(P, by_slot1, byslot1_ps)
            pe.wait_ge(byslot2_loaded, 16 * len(tables))
            pe.wait_ge(normsq_ready, BATCHES)
            by_row(S2, by_slot2, byslot2_ps)
            pe.wait_ge(experts_ready, 1)
            pe.wait_ge(up_lo_ready, 2 * EXPERTS)
            pe.wait_ge(rel_ready, BATCHES)
            pe.wait_ge(v_ready, BATCHES)
            pe.wait_ge(x1_ready, BATCHES * NT)

            down_at_w, up_at_w, next_at_w = (pe.alloc_register(n) for n in ("down_at_w", "up_at_w", "next_at_w"))

            def read_next(s):
                pe.reg_load(next_at_w, weights_at[0:1, bass.ds(s.value(), 1)])

            def transpose_x(s):
                wait(pe, xg_loaded[s.place(2)], s.before(2) * 16 + 16)
                wait(pe, xgtlo_ready, s.value())
                for c in range(DC):
                    mm = pe.transpose(xgt_ps[:, c, :], xg[:, s.place(2), c * P:(c + 1) * P], ident[:, :])
                mm.then_inc(xgt_done, 1)

            read_next(Index(0))
            pe.reg_mov(up_at_w, 0)
            transpose_x(Index(0))

            def expert_step(s):
                d = s - 1
                pe.reg_mov(down_at_w, up_at_w)
                pe.reg_mov(up_at_w, next_at_w)
                if d.within(SLOTS):
                    wait(pe, h_ready, d.value(1, 1))
                    wait(pe, htlo_ready, d.value())
                    for c in range(HC):
                        mm = pe.transpose(ht_ps[:, c, :], h[:, c * P:(c + 1) * P], ident[:, :])
                    mm.then_inc(ht_done, 1)
                if s.within(SLOTS):
                    w = pe.snap(up_at_w, min_val=0, max_val=(EXPERTS - 1) * DC * HID)
                    wait(pe, xgtlo_ready, s.value(1, 1))
                    wait(pe, silu_ready, s.value())
                    for c in range(DC):
                        cols = bass.ds(w + c * HID, HID)
                        mm = product(up1_ps[:, :], (xgt_hi[:, c, :], xgt_lo[:, c, :]), (w1_hi[:, cols], w1_lo[:, cols]),
                                     c == 0, c == DC - 1)
                    mm.then_inc(up1_done, 1)
                    wait(pe, h_ready, s.value())
                    for c in range(DC):
                        cols = bass.ds(w + c * HID, HID)
                        mm = product(up3_ps[:, :], (xgt_hi[:, c, :], xgt_lo[:, c, :]), (w3_hi[:, cols], w3_lo[:, cols]),
                                     c == 0, c == DC - 1)
                    mm.then_inc(up3_done, 1)
                if (s + 1).within(SLOTS):
                    transpose_x(s + 1)
                    read_next(s + 1)
                if d.within(SLOTS):
                    w = pe.snap(down_at_w, min_val=0, max_val=(EXPERTS - 1) * HC * D)
                    if d.i is None and d.base == 0:
                        pe.wait_ge(down_lo_ready, EXPERTS)
                    wait(pe, htlo_ready, d.value(1, 1))
                    wait(pe, y_ready, d.value())
                    for c in range(HC):
                        cols = bass.ds(w + c * D, D)
                        mm = product(down_ps, (ht_hi[:, c, :], ht_lo[:, c, :]), (w2_hi[:, cols], w2_lo[:, cols]),
                                     c == 0, c == HC - 1)
                    mm.then_inc(down_done, 1)

            expert_steps(pe, expert_step)


def kernel(x, adj, L0_gnn_Wq, L0_gnn_Wk, L0_gnn_Wv, L0_ffn_Wg, L0_ffn_bg, L0_ffn_W1, L0_ffn_W3, L0_ffn_W2):
    import numpy as np
    import concourse.bacc as bacc
    from concourse.bass_utils import run_bass_kernel_spmd

    given = {"x": x, "adj": adj, "w_q": L0_gnn_Wq, "w_k": L0_gnn_Wk, "w_v": L0_gnn_Wv, "w_gate": L0_ffn_Wg,
             "b_gate": L0_ffn_bg, "w_1": L0_ffn_W1, "w_3": L0_ffn_W3, "w_2": L0_ffn_W2}
    nc = bacc.Bacc("TRN2", target_bir_lowering=False, num_devices=1)
    arrays, args = {}, []
    for name, a in given.items():
        a = np.ascontiguousarray(a)
        arrays[f"in_{name}"] = a
        args.append(nc.dram_tensor(f"in_{name}", a.shape, mybir.dt.from_np(a.dtype), kind="ExternalInput").ap())
    batches, nodes, d = x.shape
    out = nc.dram_tensor("out", (batches * nodes + P, d), F32, kind="ExternalOutput").ap()
    graph_and_experts(nc, *args, out)
    r = run_bass_kernel_spmd(nc, [arrays], core_ids=[0])
    return r.results[0]["out"][:batches * nodes].reshape(batches, nodes, d)
```

```python
from contextlib import ExitStack

import concourse.bass as bass
from concourse import mybir

ALU = mybir.AluOpType
ACT = mybir.ActivationFunctionType
F32 = mybir.dt.float32
F32R = mybir.dt.float32r
BF16 = mybir.dt.bfloat16
I32 = mybir.dt.int32
U32 = mybir.dt.uint32
AX_X = mybir.AxisListType.X

P = 128
EPS = 1e-5
TOP_K = 2
UNROLL = 4


class Index:

    def __init__(self, base, i=None, unroll=1):
        self.base, self.i, self.unroll = base, i, unroll

    def __add__(self, n):
        return Index(self.base + n, self.i, self.unroll)

    def __sub__(self, n):
        return self + (-n)

    def value(self, scale=1, plus=0):
        if self.i is None:
            return scale * self.base + plus
        return self.i * (scale * self.unroll) + (scale * self.base + plus)

    def before(self, ring=1):
        if self.i is None:
            return self.base // ring
        return self.i * (self.unroll // ring) + self.base // ring

    def place(self, ring):
        return self.base % ring

    def within(self, n):
        return self.i is not None or 0 <= self.base < n


def steps(eng, first, last, rolled_first, rolled_last, unroll, body):
    for k in range(first, rolled_first):
        body(Index(k))
    count = (rolled_last - rolled_first + 1) // unroll
    with eng.Fori(0, count) as i:
        for u in range(unroll):
            body(Index(rolled_first + u, i, unroll))
    for k in range(rolled_first + count * unroll, last + 1):
        body(Index(k))


def wait(eng, sem, count):
    if isinstance(count, int):
        if count <= 0:
            return
    else:
        assert count.min_val > 0
    eng.wait_ge(sem, count)


def hold(eng, held):
    eng.sem_inc(held, 1)


def graph_and_experts(nc, x, adj, w_q, w_k, w_v, w_gate, b_gate, w_1, w_3, w_2, out):
    BATCHES, NODES, D = x.shape
    EXPERTS, _, HID = w_1.shape
    TOKENS = BATCHES * NODES
    NT = NODES // P
    DC = D // P
    HC = HID // P
    TILES = TOKENS // P
    SLOTS = (TOP_K * TOKENS + EXPERTS * (P - 1)) // P
    ROWS = EXPERTS * TILES + (SLOTS - TOP_K * TILES)
    SPARE = ROWS * P
    TABLE = SPARE + P
    assert DC == NT == 2 and HID <= 512 and SLOTS > P and TABLE % P == 0
    S2 = SLOTS - P
    WEIGHTS = DC * HID
    assert WEIGHTS == HC * D

    ctx = ExitStack()
    with ctx:
        def sem(name):
            return ctx.enter_context(nc.semaphore(name))

        def sems(name, n):
            return [sem(f"{name}{i}") for i in range(n)]

        bank = [ctx.enter_context(nc.psum_tensor(f"bank{i}", [P, 512], F32)) for i in range(8)]
        tables = [nc.dram_tensor(f"table{j}", (TABLE, 2), F32, kind="Internal").ap() for j in range(TOP_K * NT)]
        tokens_dram = nc.dram_tensor("tokens", (TOKENS + P, D), F32, kind="Internal").ap()

        ALIGN = 32
        first_byte = -(-nc.sbuf_base // ALIGN) * ALIGN

        class Area:

            def __init__(self, start, size):
                self.at, self.end = start, start + size

            def __call__(self, name, shape, dt=F32):
                n = mybir.dt.size(dt)
                for m in shape[1:]:
                    n *= m
                t = nc.alloc_sbuf_tensor_at(name, shape, dt, offset=self.at)
                self.at += -(-n // ALIGN) * ALIGN
                assert self.at <= self.end, (name, self.at - self.end)
                return t

        UP = EXPERTS * DC * HID * 4
        DOWN = EXPERTS * HC * D * 4
        LAST = DOWN // EXPERTS
        SLOT = (2 * D + 2 * DC * P + HID + 2 * HC * P + 2 * D) * 4
        up_area = Area(first_byte, 4 * UP)
        down_at = up_area.end
        slot_at = down_at + 2 * DOWN
        keep = Area(slot_at + SLOT, nc.sbuf_usable_end - slot_at - SLOT)

        def weights(name, area, n):
            hi = area(f"{name}_hi", [P, n], F32R)
            at = area.at
            lo = area(f"{name}_lo", [P, n], F32R)
            raw = Area(at, n * 4)(f"{name}_raw", [P, n])
            return hi, lo, raw

        up_hi, up_lo, up_raw = weights("up", up_area, 2 * UP // 4)
        w2_hi, w2_lo, w2_raw = weights("w2", Area(down_at, 2 * DOWN), DOWN // 4)

        area = Area(slot_at, SLOT)
        xg = area("xg", [P, 2, D])
        xgt_hi = area("xgt_hi", [P, DC, P], F32R)
        xgt_lo = area("xgt_lo", [P, DC, P], F32R)
        h = area("h", [P, HID])
        ht_hi = area("ht_hi", [P, HC, P], F32R)
        late_at = area.at
        ht_lo = area("ht_lo", [P, HC, P], F32R)
        y = area("y", [P, 2, D])
        area = Area(slot_at, late_at - slot_at)
        by_slot1 = area("by_slot1", [P, TOP_K * NT, P, 2])
        is_pad1 = area("is_pad1", [P, P])
        expert_f = area("expert_f", [1, SLOTS])
        by_slot2 = Area(late_at, slot_at + SLOT - late_at)("by_slot2", [S2, TOP_K * NT, P, 2])
        first = Area(slot_at, late_at - slot_at)
        zero_rows = first("zero_rows", [P, D])
        blank = first("blank", [P, TABLE // P, 2])
        assert area.at <= first.at
        slot_free = first("slot_free", [1, SLOTS])

        ER = 4
        ident = keep("ident", [P, P])
        ids = keep("ids", [P, SLOTS], U32)
        gates = keep("gates", [P, SLOTS])
        weights_at = keep("weights_at", [1, SLOTS], I32)
        gather_id = keep("gather_id", [P, 2], U32)
        scatter_id = keep("scatter_id", [P, 2], U32)
        first_free = keep("first_free", [P, EXPERTS])
        start_row = keep("start_row", [P, EXPERTS])
        entry = keep("entry", [P, ER, TOP_K, NT, 2])
        row_u = keep("row_u", [P, ER, TOP_K * NT], U32)
        is_pad2 = keep("is_pad2", [P, S2])
        pad_id = keep("pad_id", [P, 1])
        slot_no = keep("slot_no", [P, 2])
        all_ones = keep("all_ones", [P, EXPERTS])
        count_i = keep("count_i", [P, EXPERTS], I32)
        slots_i = keep("slots_i", [P, EXPERTS], I32)
        slots_of = keep("slots_of", [P, EXPERTS])
        slots_end = keep("slots_end", [P, EXPERTS])
        slot_gap = keep("slot_gap", [P, EXPERTS])
        past = keep("past", [P, 2, EXPERTS])
        skipped = keep("skipped", [P, 2, EXPERTS])
        table_row = keep("table_row", [P, 2])
        table_row_u = keep("table_row_u", [P, 2], U32)

        XR = 4
        small = Area(down_at, DOWN - LAST)
        x_in = small("x_in", [P, XR, NT, D])
        x1 = small("x1", [P, 2, NT, D])
        v = small("v", [P, NT, D])
        rel = small("rel", [P, NT, NODES])
        rel_sq = small("rel_sq", [P, NT, NODES])
        sq_sum = small("sq_sum", [P, NODES])
        adj_sb = small("adj_sb", [P, NT, NODES])
        wq_sb = small("wq_sb", [P, DC, D])
        wk_sb = small("wk_sb", [P, DC, D])
        wv_sb = small("wv_sb", [P, DC, D])
        area = Area(down_at + DOWN, DOWN - LAST)
        xn = area("xn", [P, 2, NT, D])
        xnt_hi = area("xnt_hi", [P, 2, DC, NODES], F32R)
        xnt_lo = area("xnt_lo", [P, 2, DC, NODES], F32R)
        g_hi = area("g_hi", [P, DC, NODES], F32R)
        g_lo = area("g_lo", [P, DC, NODES], F32R)
        at_hi = area("at_hi", [P, DC, D], F32R)
        at_lo = area("at_lo", [P, DC, D], F32R)
        wvt_hi = area("wvt_hi", [P, DC, D], F32R)
        wvt_lo = area("wvt_lo", [P, DC, D], F32R)
        half = small("half", [P, NT])
        part1 = small("part1", [P, NT, 6])
        mean1 = small("mean1", [P, 2, NT, 2])
        var1 = small("var1", [P, 2, NT])
        rstd1 = small("rstd1", [P, 2, NT])
        shift1 = small("shift1", [P, 2, NT])
        norm_sq = small("norm_sq", [P, NT])
        norm_inv = small("norm_inv", [P, NT])
        part2 = small("part2", [P, NT, 6])
        mean2 = small("mean2", [P, NT, 2])
        var2 = small("var2", [P, NT])
        rstd2 = small("rstd2", [P, NT])
        shift2 = small("shift2", [P, NT])
        ones_col = small("ones_col", [P, 1])

        area = Area(down_at + DOWN - LAST, LAST)
        xn2 = area("xn2", [P, 2, NT, D])
        area = Area(down_at + 2 * DOWN - LAST, LAST)
        xn2_t = area("xn2_t", [P, DC, NODES])
        wg_sb = area("wg_sb", [P, DC, EXPERTS])
        bg_sb = area("bg_sb", [P, EXPERTS])
        before = area("before", [P, P], BF16)
        ones = area("ones", [P, P], BF16)
        token_no = area("token_no", [P, TILES])
        expert_no = area("expert_no", [P, EXPERTS])
        spare_row = area("spare_row", [P, 1])
        logit = area("logit", [P, NT, EXPERTS])
        top = area("top", [P, NT, 8])
        top_at = area("top_at", [P, NT, 8], U32)
        top_no = area("top_no", [P, TOP_K, NT])
        chosen = area("chosen", [P, TOP_K, NT, EXPERTS])
        either = area("either", [P, NT, EXPERTS], BF16)
        margin = area("margin", [P, NT])
        rank = area("rank", [P, NT, EXPERTS])
        picked = area("picked", [P, TOP_K * NT, EXPERTS])
        row = area("row", [P, TOP_K * NT])

        held_dve = sem("held_dve")
        held_pool = sem("held_pool")
        x_loaded = sems("x_loaded", XR)
        wqk_loaded = sem("wqk_loaded")
        wv_loaded = sem("wv_loaded")
        gate_w_loaded = sem("gate_w_loaded")
        up_loaded = sem("up_loaded")
        up_rest_loaded = sem("up_rest_loaded")
        down_loaded = sems("down_loaded", EXPERTS)
        up_hi_ready = sem("up_hi_ready")
        up_lo_ready = sem("up_lo_ready")
        down_hi_ready = sem("down_hi_ready")
        down_lo_ready = sem("down_lo_ready")
        adj_loaded = sem("adj_loaded")
        ident_zero = sem("ident_zero")
        ident_made = sem("ident_made")
        before_made = sem("before_made")
        iotas_made = sem("iotas_made")
        zeros_made = sem("zeros_made")
        consts_made = sem("consts_made")
        blank_made = sem("blank_made")
        blank_stored = sem("blank_stored")
        spare_stored = sem("spare_stored")
        a_done = sem("a_done")
        wvt_done = sem("wvt_done")
        a_hi_ready = sem("a_hi_ready")
        a_lo_ready = sem("a_lo_ready")
        wvt_hi_ready = sem("wvt_hi_ready")
        wvt_lo_ready = sem("wvt_lo_ready")

        part1_ready = sem("part1_ready")
        mean1_ready = sem("mean1_ready")
        var1_ready = sem("var1_ready")
        rstd1_ready = sem("rstd1_ready")
        xn_ready = sem("xn_ready")
        xnt_done = sem("xnt_done")
        xnthi_ready = sem("xnthi_ready")
        xntlo_ready = sem("xntlo_ready")
        shift1_ready = sem("shift1_ready")
        g_done = sem("g_done")
        ghi_ready = sem("ghi_ready")
        glo_ready = sem("glo_ready")
        v_done = sem("v_done")
        v_ready = sem("v_ready")
        rel_done = sem("rel_done")
        rel_ready = sem("rel_ready")
        relsq_ready = sem("relsq_ready")
        sqsum_ready = sem("sqsum_ready")
        mix_done = sem("mix_done")
        norm_done = sem("norm_done")
        normsq_ready = sem("normsq_ready")
        norminv_ready = sem("norminv_ready")
        x1_ready = sem("x1_ready")
        x1_stored = sems("x1_stored", 2)
        part2_ready = sem("part2_ready")
        mean2_ready = sem("mean2_ready")
        var2_ready = sem("var2_ready")
        rstd2_ready = sem("rstd2_ready")
        shift2_ready = sem("shift2_ready")
        xn2_ready = sem("xn2_ready")
        xn2_stored = sems("xn2_stored", 2)
        xn2t_done = sem("xn2t_done")
        xn2t_ready = sem("xn2t_ready")
        logit_done = sem("logit_done")
        logit_ready = sem("logit_ready")
        top_ready = sem("top_ready")
        topat_ready = sem("topat_ready")
        topno_ready = sem("topno_ready")
        chosen_ready = sem("chosen_ready")
        either_ready = sem("either_ready")
        margin_ready = sem("margin_ready")
        prefix_done = sem("prefix_done")
        rank_ready = sem("rank_ready")
        free_ready = sem("free_ready")
        picked_ready = sem("picked_ready")
        row_ready = sem("row_ready")
        rowu_ready = sem("rowu_ready")
        gate_ready = sem("gate_ready")
        id_ready = sem("id_ready")
        entries_stored = sems("entries_stored", TOP_K * NT)

        plan = sem("plan")
        tablerow_ready = sem("tablerow_ready")
        experts_ready = sem("experts_ready")
        byslot1_loaded = sems("byslot1_loaded", TOP_K * NT)
        byslot2_loaded = sems("byslot2_loaded", TOP_K * NT)
        byslot_done = sem("byslot_done")
        ids_ready = sem("ids_ready")
        gates_ready = sem("gates_ready")

        gid_ready = sem("gid_ready")
        sid_ready = sem("sid_ready")
        xg_loaded = sems("xg_loaded", 2)
        xgt_done = sem("xgt_done")
        xgthi_ready = sem("xgthi_ready")
        xgtlo_ready = sem("xgtlo_ready")
        up1_done = sem("up1_done")
        up3_done = sem("up3_done")
        silu_ready = sem("silu_ready")
        h_ready = sem("h_ready")
        ht_done = sem("ht_done")
        hthi_ready = sem("hthi_ready")
        htlo_ready = sem("htlo_ready")
        down_done = sem("down_done")
        y_ready = sem("y_ready")
        y_added = sem("y_added")

        xnt_ps = bank[0][:, :].rearrange("p (c n) -> p c n", c=DC)
        g_ps = bank[1][:, :].rearrange("p (c n) -> p c n", c=DC)
        v_ps = bank[2][:, :].rearrange("p (t n) -> p t n", t=NT)
        rel_ps = bank[3][:, :].rearrange("p (t n) -> p t n", t=NT)
        mix_ps = bank[4][:, :].rearrange("p (t n) -> p t n", t=NT)
        xn2t_ps = bank[5][:, :].rearrange("p (c n) -> p c n", c=DC)
        norm_ps = bank[6][:, 0:NT]
        RE = NT * EXPERTS
        logit_ps = bank[7][:, 0:RE].rearrange("p (t e) -> p t e", t=NT)
        rank_ps = bank[6][:, 64:64 + RE].rearrange("p (t e) -> p t e", t=NT)
        count_ps = bank[6][:, 64 + RE:64 + RE + EXPERTS]
        byslot1_ps = [bank[5 + c][:, 128:128 + P] for c in range(2)]
        byslot2_ps = [bank[6 + c][:, 256:256 + S2] for c in range(2)]
        up1_ps, up3_ps = bank[0], bank[1]
        ht_ps = bank[2][:, :].rearrange("p (c n) -> p c n", c=HC)
        xgt_ps = bank[3][:, 0:DC * P].rearrange("p (c n) -> p c n", c=DC)
        down_ps = bank[4][:, 0:D]

        x_rows = x.rearrange("b (t p) d -> (b t) p d", p=P)
        out_rows = out.rearrange("(r p) d -> r p d", p=P)
        token_rows = tokens_dram.rearrange("(r p) d -> r p d", p=P)

        def batch_rows(rows, b):
            return rows[bass.ds(b.value(NT), NT), :, :].rearrange("t p d -> p t d")

        LAG = 6
        G_ROLL = (LAG + 3, LAG + 2 + (BATCHES - LAG - 4) // UNROLL * UNROLL)
        PIECE = 2 * EXPERTS * WEIGHTS // BATCHES
        assert PIECE * BATCHES == 2 * EXPERTS * WEIGHTS
        UP_FIRST, UP_SOON = 2 * EXPERTS - 9, 2
        assert UP_SOON < UP_FIRST and UP_SOON * WEIGHTS // PIECE - 1 + 5 < G_ROLL[0]

        def up_piece(u, t):
            return t[:, bass.ds(u.value(PIECE), PIECE)]

        def down_piece(e, *of):
            return [t[:, e * HC * D:(e + 1) * HC * D] for t in of]

        down_loads = {BATCHES + 2: range(0, 2), BATCHES + 3: range(2, 5), BATCHES + 4: range(5, EXPERTS - 1)}
        down_splits = {BATCHES + 3: range(0, 2)}

        def graph_steps(eng, body):
            steps(eng, 0, BATCHES - 1 + LAG, *G_ROLL, UNROLL, body)

        E_ROLL = (3, 3 + (SLOTS - 4) // UNROLL * UNROLL - 1)

        def expert_steps(eng, body):
            steps(eng, 0, SLOTS, *E_ROLL, UNROLL, body)

        block = ctx.enter_context(nc.Block())

        @block.sync
        def _(sp):
            def load_x(b):
                sp.dma_start(x_in[:, b.place(XR)], batch_rows(x_rows, b)).then_inc(x_loaded[b.place(XR)], 16)

            def load_w(w, to, loaded):
                sp.dma_start(to[:, :, :], w.rearrange("(c p) d -> p c d", p=P)).then_inc(loaded, 16)

            load_w(w_q, wq_sb, wqk_loaded)
            load_w(w_k, wk_sb, wqk_loaded)
            load_x(Index(0))
            load_w(w_v, wv_sb, wv_loaded)
            sp.dma_start(adj_sb[:, :, :], adj.rearrange("(t p) n -> p t n", p=P)).then_inc(adj_loaded, 16)
            for b in range(1, XR):
                load_x(Index(b))
            sp.dma_start(wg_sb[:, :, :], w_gate.rearrange("(c p) e -> p c e", p=P)).then_inc(gate_w_loaded, 16)
            sp.dma_start(bg_sb[:, :], b_gate.partition_broadcast(P)).then_inc(gate_w_loaded, 16)
            sp.wait_ge(zeros_made, 1)
            sp.dma_start(token_rows[TILES], zero_rows[:, :]).then_inc(spare_stored, 16)
            sp.dma_start(out_rows[TILES], zero_rows[:, :]).then_inc(spare_stored, 16)
            sp.wait_ge(blank_made, 1)
            for table in tables:
                sp.dma_start(table.rearrange("(p j) c -> p j c", p=P), blank[:, :, :]).then_inc(blank_stored, 16)

            def load_up(n, loaded):
                sp.dma_start(up_raw[:, n * WEIGHTS:(n + 1) * WEIGHTS].rearrange("p (c n) -> p c n", c=DC),
                             (w_1, w_3)[n // EXPERTS][n % EXPERTS].rearrange("(c p) n -> p c n", p=P)) \
                    .then_inc(loaded, 16)

            up_rest = {3 + i: range(UP_FIRST + 3 * i, UP_FIRST + 3 * i + 3) for i in range(3)}
            for n in range(UP_FIRST):
                load_up(n, up_loaded)

            def load_down(e):
                if e >= 2:
                    sp.wait_ge(down_loaded[e - 2], 16)
                (to,) = down_piece(e, w2_raw)
                sp.dma_start(to.rearrange("p (c n) -> p c n", c=HC),
                             w_2[e].rearrange("(c p) n -> p c n", p=P)).then_inc(down_loaded[e], 16)

            def step(k):
                b = k - 3
                if b.within(BATCHES):
                    wait(sp, x1_ready, b.value(NT, NT))
                    sp.dma_start(batch_rows(out_rows, b), x1[:, b.place(2)]).then_inc(x1_stored[b.place(2)], 16)
                nxt = k + 1
                if nxt.within(BATCHES) and (nxt.i is not None or nxt.base >= XR):
                    load_x(nxt)
                if k.i is None:
                    for n in up_rest.get(k.base, []):
                        load_up(n, up_rest_loaded)
                    for e in down_loads.get(k.base, []):
                        if e == 0:
                            sp.wait_ge(rel_done, BATCHES)
                        load_down(e)
                if b.within(BATCHES):
                    wait(sp, xn2_ready, b.value(NT, NT))
                    sp.dma_start(batch_rows(token_rows, b), xn2[:, b.place(2)]).then_inc(xn2_stored[b.place(2)], 16)

            graph_steps(sp, step)

            sp.wait_ge(rowu_ready, BATCHES)
            sp.wait_ge(id_ready, BATCHES * TOP_K)
            sp.wait_ge(gate_ready, BATCHES * TOP_K)
            load_down(EXPERTS - 1)

        @block.gpsimd
        def _(pool):
            pool.memset(ident[:, :], 0.0).then_inc(ident_zero, 1)
            pool.memset(before[:, :], 1.0).then_inc(ident_zero, 1)
            pool.wait_ge(ident_zero, 2)
            pool.affine_select(out=ident[:, :], in_=ident[:, :], compare_op=ALU.not_equal, fill=1.0, base=0,
                               pattern=[[-1, P]], channel_multiplier=1).then_inc(ident_made, 1)
            pool.affine_select(out=before[:, :], in_=before[:, :], compare_op=ALU.is_gt, fill=0.0, base=0,
                               pattern=[[1, P]], channel_multiplier=-1).then_inc(before_made, 1)
            pool.memset(zero_rows[:, :], 0.0).then_inc(zeros_made, 1)
            pool.memset(half[:, :], -0.5).then_inc(iotas_made, 1)
            pool.iota(expert_no[:, :], [[1, EXPERTS]], base=0, channel_multiplier=0,
                      allow_small_or_imprecise_dtypes=True).then_inc(iotas_made, 1)
            pool.iota(start_row[:, :], [[TOKENS, EXPERTS]], base=-SPARE, channel_multiplier=-1,
                      allow_small_or_imprecise_dtypes=True).then_inc(iotas_made, 1)
            pool.iota(spare_row[:, :], [[0, 1]], base=SPARE, channel_multiplier=1,
                      allow_small_or_imprecise_dtypes=True).then_inc(iotas_made, 1)
            pool.iota(token_no[:, :], [[P, TILES]], base=1, channel_multiplier=1,
                      allow_small_or_imprecise_dtypes=True).then_inc(iotas_made, 1)
            pool.iota(slot_no[:, :], [[P, 2]], base=0, channel_multiplier=1,
                      allow_small_or_imprecise_dtypes=True).then_inc(iotas_made, 1)
            pool.iota(slot_free[:, :], [[1, SLOTS]], base=0, channel_multiplier=0,
                      allow_small_or_imprecise_dtypes=True).then_inc(iotas_made, 1)
            pool.iota(pad_id[:, :], [[0, 1]], base=TOKENS + 1, channel_multiplier=1,
                      allow_small_or_imprecise_dtypes=True).then_inc(iotas_made, 1)

            def store_entries(c, kk):
                q = c.place(ER)
                for t in range(NT):
                    j = kk * NT + t
                    wait(pool, entries_stored[j], c.value(16))
                    hold(pool, held_pool)
                    pool.indirect_dma_start(
                        tables[j][:, :], bass.IndirectOffsetOnAxis(row_u[:, q, j:j + 1], 0),
                        entry[:, q, kk, t, :], None).then_inc(entries_stored[j], 16)

            def step(k):
                b = k - 3
                if b.within(BATCHES):
                    wait(pool, normsq_ready, b.value(1, 1))
                    wait(pool, x1_ready, b.value(NT))
                    pool.tensor_tensor(norm_inv[:, :], norm_sq[:, :], half[:, :], ALU.pow).then_inc(norminv_ready, 1)
                if k.within(BATCHES):
                    if k.i is None and k.base == 0:
                        pool.wait_ge(iotas_made, 8)
                    wait(pool, var1_ready, k.value(1, 1))
                    wait(pool, xn_ready, (k - 1).value(NT))
                    pool.tensor_tensor(rstd1[:, k.place(2)], var1[:, k.place(2)], half[:, :],
                                       ALU.pow).then_inc(rstd1_ready, 1)
                r = k - 5
                if r.within(BATCHES):
                    for stored in entries_stored:
                        wait(pool, stored, (r - ER + 1).value(16))
                    for kk in range(TOP_K):
                        pool.tensor_copy(entry[:, r.place(ER), kk, :, 0], token_no[:, bass.ds(r.value(NT), NT)]) \
                            .then_inc(id_ready, 1)
                c = k - 6
                if c.within(BATCHES):
                    wait(pool, id_ready, c.value(TOP_K, TOP_K))
                    wait(pool, gate_ready, c.value(TOP_K, TOP_K))
                    wait(pool, rowu_ready, c.value(1, 1))
                    if c.i is None and c.base == 0:
                        pool.wait_ge(blank_stored, 16 * len(tables))
                    store_entries(c, 0)
                if b.within(BATCHES):
                    wait(pool, var2_ready, b.value(1, 1))
                    wait(pool, xn2_ready, b.value(NT))
                    pool.tensor_tensor(rstd2[:, :], var2[:, :], half[:, :], ALU.pow).then_inc(rstd2_ready, 1)
                if c.within(BATCHES):
                    store_entries(c, 1)

            graph_steps(pool, step)

            def gather_entries(n, at, to, loaded):
                for j, table in enumerate(tables):
                    pool.wait_ge(entries_stored[j], 16 * BATCHES)
                    pool.indirect_dma_start(to[:, j].rearrange("s p c -> s (p c)"), None,
                                            table.rearrange("(r p) c -> r (p c)", p=P),
                                            bass.IndirectOffsetOnAxis(at, 0)).then_inc(loaded[j], 16)

            pool.wait_ge(tablerow_ready, 1)
            pool.wait_ge(blank_stored, 16 * len(tables))
            gather_entries(P, table_row_u[0:P, 0:1], by_slot1, byslot1_loaded)
            for q in range(2):
                pool.wait_ge(xn2_stored[q], BATCHES // 2 * 16)
                pool.wait_ge(x1_stored[q], BATCHES // 2 * 16)
            pool.wait_ge(spare_stored, 32)
            pool.wait_ge(ids_ready, 1)

            def gather(s):
                q = s.place(2)
                wait(pool, xgt_done, (s - 1).value())
                pool.tensor_copy(gather_id[:, q:q + 1], ids[:, bass.ds(s.value(), 1)]).then_inc(gid_ready, 1)
                wait(pool, gid_ready, s.value(1, 1))
                hold(pool, held_pool)
                pool.indirect_dma_start(xg[:, q, :], None, tokens_dram[:, :],
                                        bass.IndirectOffsetOnAxis(gather_id[:, q:q + 1], 0)) \
                    .then_inc(xg_loaded[q], 16)

            def add(s):
                q = s.place(2)
                wait(pool, y_added, (s - 1).value(16))
                pool.tensor_copy(scatter_id[:, q:q + 1], ids[:, bass.ds(s.value(), 1)]).then_inc(sid_ready, 1)
                wait(pool, sid_ready, s.value(1, 1))
                wait(pool, y_added, s.value(16))
                wait(pool, y_ready, s.value(1, 1))
                hold(pool, held_pool)
                pool.indirect_dma_start(out[:, :], bass.IndirectOffsetOnAxis(scatter_id[:, q:q + 1], 0),
                                        y[:, q, :], None, compute_op=ALU.add).then_inc(y_added, 16)

            gather(Index(0))
            gather(Index(1))
            gather_entries(S2, table_row_u[0:S2, 1:2], by_slot2, byslot2_loaded)

            def expert_step(s):
                if s.i is None and s.base == 1:
                    pool.wait_ge(ids_ready, 2)
                if (s + 2).within(SLOTS):
                    gather(s + 2)
                if (s - 1).within(SLOTS):
                    add(s - 1)

            steps(pool, 0, SLOTS, 3, 3 + (SLOTS - 4) // 2 * 2 - 1, 2, expert_step)
            pool.wait_ge(y_added, 16 * SLOTS)

        @block.scalar
        def _(act):
            def split_down(e):
                hi, raw = down_piece(e, w2_hi, w2_raw)
                act.wait_ge(down_loaded[e], 16)
                if e == 0:
                    for q in range(2):
                        act.wait_ge(x1_stored[q], BATCHES // 2 * 16)
                if e == EXPERTS - 1:
                    for q in range(2):
                        act.wait_ge(xn2_stored[q], BATCHES // 2 * 16)
                    act.wait_ge(xn2t_done, BATCHES)
                act.copy(hi, raw).then_inc(down_hi_ready, 1)

            def step(k):
                r = k - 5
                if r.within(BATCHES):
                    if r.i is None and r.base == 0:
                        act.wait_ge(up_loaded, 16 * UP_FIRST)
                    if r.i is None and (r + 1).base * PIECE == UP_SOON * WEIGHTS:
                        act.wait_ge(up_rest_loaded, 16 * (2 * EXPERTS - UP_FIRST))
                    act.copy(up_piece(r, up_hi), up_piece(r, up_raw)).then_inc(up_hi_ready, 1)
                m = k - 2
                if m.within(BATCHES):
                    wait(act, g_done, m.value(1, 1))
                    wait(act, rel_done, m.value())
                    act.copy(g_hi[:, :, :], g_ps).then_inc(ghi_ready, 1)
                    wait(act, v_done, m.value(1, 1))
                    wait(act, mix_done, m.value())
                    act.copy(v[:, :, :], v_ps).then_inc(v_ready, 1)
                b = k - 4
                if b.within(BATCHES):
                    wait(act, xn2t_done, b.value(1, 1))
                    wait(act, logit_done, b.value())
                    act.copy(xn2_t[:, :, :], xn2t_ps).then_inc(xn2t_ready, 1)
                r = k - 5
                if r.within(BATCHES):
                    wait(act, margin_ready, r.value(1, 1))
                    wait(act, id_ready, r.value(TOP_K, TOP_K))
                    for kk, sign in ((0, 1.0), (1, -1.0)):
                        act.activation(entry[:, r.place(ER), kk, :, 1], margin[:, :], ACT.Sigmoid,
                                       scale=sign).then_inc(gate_ready, 1)
                if k.i is None and k.base == 1:
                    act.wait_ge(a_done, 1)
                    act.copy(at_hi[:, :, :], g_ps).then_inc(a_hi_ready, 1)
                    act.wait_ge(wvt_done, 1)
                    act.copy(wvt_hi[:, :, :], v_ps).then_inc(wvt_hi_ready, 1)
                if k.within(BATCHES):
                    q = k.place(2)
                    wait(act, shift1_ready, k.value(1, 1))
                    wait(act, xnt_done, (k - 1).value())
                    for t in range(NT):
                        act.activation(xn[:, q, t, :], x_in[:, k.place(XR), t, :], ACT.Identity,
                                       bias=shift1[:, q, t:t + 1], scale=rstd1[:, q, t:t + 1]).then_inc(xn_ready, 1)
                b = k - 1
                if b.within(BATCHES):
                    wait(act, xnt_done, b.value(1, 1))
                    wait(act, rel_done, (b - 1).value())
                    act.copy(xnt_hi[:, b.place(2)], xnt_ps).then_inc(xnthi_ready, 1)
                if m.within(BATCHES):
                    wait(act, rel_ready, m.value(1, 1))
                    wait(act, sqsum_ready, m.value())
                    act.activation(rel_sq[:, :, :], rel[:, :, :], ACT.Square).then_inc(relsq_ready, 1)
                b = k - 3
                if b.within(BATCHES):
                    q = b.place(2)
                    wait(act, shift2_ready, b.value(1, 1))
                    wait(act, xn2_stored[q], b.before(2) * 16)
                    wait(act, xn2t_done, (b - 1).value())
                    for t in range(NT):
                        act.activation(xn2[:, q, t, :], x1[:, q, t, :], ACT.Identity,
                                       bias=shift2[:, t:t + 1], scale=rstd2[:, t:t + 1]).then_inc(xn2_ready, 1)
                if k.i is None:
                    for e in down_splits.get(k.base, []):
                        split_down(e)

            graph_steps(act, step)

            for e in range(2, EXPERTS):
                split_down(e)
            act.wait_ge(byslot_done, 1)
            act.copy(gates[:, 0:P], byslot1_ps[1]).then_inc(gates_ready, 1)

            def transposed(s):
                wait(act, xgt_done, s.value(1, 1))
                act.copy(xgt_hi[:, :, :], xgt_ps).then_inc(xgthi_ready, 1)

            transposed(Index(0))

            def expert_step(s):
                d = s - 1
                if d.within(SLOTS):
                    wait(act, ht_done, d.value(1, 1))
                    wait(act, down_done, d.value())
                    act.copy(ht_hi[:, :, :], ht_ps).then_inc(hthi_ready, 1)
                if s.within(SLOTS):
                    wait(act, up1_done, s.value(1, 1))
                    wait(act, ht_done, s.value())
                    act.activation(h[:, :], up1_ps[:, :], ACT.Silu).then_inc(silu_ready, 1)
                if (s + 1).within(SLOTS):
                    transposed(s + 1)
                if d.within(SLOTS):
                    wait(act, down_done, d.value(1, 1))
                    wait(act, y_added, (d - 1).value(16))
                    act.activation(y[:, d.place(2), :], down_ps, ACT.Copy,
                                   scale=gates[:, bass.ds(d.value(), 1)]).then_inc(y_ready, 1)
                if s.i is None and s.base == 0:
                    act.wait_ge(byslot_done, 2)
                    act.copy(gates[:, P:SLOTS], byslot2_ps[1]).then_inc(gates_ready, 1)
                    act.wait_ge(gates_ready, 2)

            expert_steps(act, expert_step)

        @block.vector
        def _(dve):
            dve.memset(ones[:, :], 1.0).then_inc(consts_made, 1)
            dve.memset(ones_col[:, :], 1.0).then_inc(consts_made, 1)
            dve.memset(all_ones[:, :], 1.0).then_inc(consts_made, 1)
            dve.memset(blank[:, :, :], 0.0).then_inc(blank_made, 1)
            dve.wait_ge(iotas_made, 8)
            dve.tensor_copy(first_free[:, :], start_row[:, :]).then_inc(free_ready, 1)

            def lo_of_down(e):
                hi, lo, raw = down_piece(e, w2_hi, w2_lo, w2_raw)
                dve.wait_ge(down_hi_ready, e + 1)
                dve.tensor_tensor(lo, raw, hi, ALU.subtract).then_inc(down_lo_ready, 1)

            def step(k):
                b, m, r, t_ = k - 3, k - 2, k - 5, k - 1
                q, kq, bq = t_.place(2), k.place(2), b.place(2)
                if b.within(BATCHES):
                    wait(dve, norm_done, b.value(1, 1))
                    wait(dve, norminv_ready, b.value())
                    dve.tensor_copy(norm_sq[:, :], norm_ps).then_inc(normsq_ready, 1)
                if r.within(BATCHES):
                    if r.i is None and r.base == 0:
                        dve.wait_ge(gate_w_loaded, 32)
                    wait(dve, logit_done, r.value(1, 1))
                    dve.tensor_tensor(logit[:, :, :], logit_ps,
                                      bg_sb[:, :].unsqueeze(1).to_broadcast([P, NT, EXPERTS]),
                                      ALU.add).then_inc(logit_ready, 1)
                if k.within(BATCHES):
                    wait(dve, x_loaded[k.place(XR)], k.before(XR) * 16 + 16)
                    dve.bn_stats(part1[:, 0, :], x_in[:, k.place(XR), 0, :]).then_inc(part1_ready, 1)
                if r.within(BATCHES):
                    wait(dve, logit_ready, r.value(1, 1))
                    hold(dve, held_dve)
                    for t in range(NT):
                        dve.max(top[:, t, :], logit[:, t, :]).then_inc(top_ready, 1)
                if k.within(BATCHES):
                    for t in range(1, NT):
                        dve.bn_stats(part1[:, t, :], x_in[:, k.place(XR), t, :]).then_inc(part1_ready, 1)
                if r.within(BATCHES):
                    wait(dve, top_ready, r.value(NT, NT))
                    hold(dve, held_dve)
                    for t in range(NT):
                        dve.max_index(top_at[:, t, :], top[:, t, :], logit[:, t, :]).then_inc(topat_ready, 1)
                    wait(dve, gate_ready, r.value(TOP_K))
                    dve.tensor_tensor(margin[:, :], top[:, :, 0], top[:, :, 1], ALU.subtract) \
                        .then_inc(margin_ready, 1)
                if k.within(BATCHES):
                    wait(dve, part1_ready, k.value(NT, NT))
                    wait(dve, shift1_ready, (k - 1).value())
                    hold(dve, held_dve)
                    for t in range(NT):
                        dve.bn_aggr(mean1[:, kq, t, :], part1[:, t, :]).then_inc(mean1_ready, 1)
                if r.within(BATCHES):
                    wait(dve, topat_ready, r.value(NT, NT))
                    dve.tensor_copy(top_no[:, :, :], top_at[:, :, 0:TOP_K].rearrange("p t k -> p k t")) \
                        .then_inc(topno_ready, 1)
                if k.within(BATCHES):
                    wait(dve, mean1_ready, k.value(NT, NT))
                    dve.tensor_scalar(var1[:, kq, :], mean1[:, kq, :, 1], EPS, None, ALU.add).then_inc(var1_ready, 1)
                if r.within(BATCHES):
                    wait(dve, topno_ready, r.value(1, 1))
                    for kk in range(TOP_K):
                        dve.tensor_tensor(chosen[:, kk], expert_no[:, :].unsqueeze(1).to_broadcast([P, NT, EXPERTS]),
                                          top_no[:, kk, :].unsqueeze(2).to_broadcast([P, NT, EXPERTS]),
                                          ALU.is_equal).then_inc(chosen_ready, 1)

                def residual(t):
                    if t == 0:
                        wait(dve, norminv_ready, b.value(1, 1))
                        wait(dve, mix_done, b.value(1, 1))
                        wait(dve, x1_stored[bq], b.before(2) * 16)
                        wait(dve, xn2_ready, (b - 1).value(NT))
                    dve.scalar_tensor_tensor(x1[:, bq, t, :], mix_ps[:, t, :], norm_inv[:, t:t + 1],
                                             x_in[:, b.place(XR), t, :], ALU.mult, ALU.add) \
                        .then_inc(x1_ready, 1)

                if b.within(BATCHES):
                    residual(0)
                if r.within(BATCHES):
                    wait(dve, chosen_ready, r.value(TOP_K, TOP_K))
                    wait(dve, prefix_done, r.value())
                    dve.tensor_tensor(either[:, :, :], chosen[:, 0], chosen[:, 1], ALU.add).then_inc(either_ready, 1)
                if m.within(BATCHES):
                    wait(dve, ghi_ready, m.value(1, 1))
                    dve.tensor_tensor(g_lo[:, :, :], g_ps, g_hi[:, :, :], ALU.subtract).then_inc(glo_ready, 1)
                if b.within(BATCHES):
                    residual(1)
                if k.within(BATCHES):
                    wait(dve, rstd1_ready, k.value(1, 1))
                    dve.scalar_tensor_tensor(shift1[:, kq, :], mean1[:, kq, :, 0], -1.0, rstd1[:, kq, :],
                                             ALU.mult, ALU.mult).then_inc(shift1_ready, 1)
                if k.i is None and k.base == 1:
                    dve.wait_ge(a_hi_ready, 1)
                    dve.tensor_tensor(at_lo[:, :, :], g_ps, at_hi[:, :, :], ALU.subtract).then_inc(a_lo_ready, 1)
                    dve.wait_ge(wvt_hi_ready, 1)
                    dve.tensor_tensor(wvt_lo[:, :, :], v_ps, wvt_hi[:, :, :], ALU.subtract).then_inc(wvt_lo_ready, 1)
                if b.within(BATCHES):
                    wait(dve, x1_ready, b.value(NT, NT))
                    for t in range(NT):
                        dve.bn_stats(part2[:, t, :], x1[:, bq, t, :]).then_inc(part2_ready, 1)
                if r.within(BATCHES):
                    wait(dve, prefix_done, r.value(1, 1))
                    wait(dve, free_ready, r.value(1, 1))
                    dve.tensor_tensor(rank[:, :, :], rank_ps,
                                      first_free[:, :].unsqueeze(1).to_broadcast([P, NT, EXPERTS]),
                                      ALU.add).then_inc(rank_ready, 1)
                if b.within(BATCHES):
                    wait(dve, part2_ready, b.value(NT, NT))
                    wait(dve, shift2_ready, b.value())
                    hold(dve, held_dve)
                    for t in range(NT):
                        dve.bn_aggr(mean2[:, t, :], part2[:, t, :]).then_inc(mean2_ready, 1)
                if b.within(BATCHES):
                    wait(dve, mean2_ready, b.value(NT, NT))
                    wait(dve, rstd2_ready, b.value())
                    dve.tensor_scalar(var2[:, :], mean2[:, :, 1], EPS, None, ALU.add).then_inc(var2_ready, 1)
                if m.within(BATCHES):
                    if m.i is None and m.base == 0:
                        dve.wait_ge(adj_loaded, 16)
                    wait(dve, rel_done, m.value(1, 1))
                    wait(dve, mix_done, m.value())
                    wait(dve, relsq_ready, m.value())
                    dve.tensor_tensor(rel[:, :, :], rel_ps, adj_sb[:, :, :], ALU.mult).then_inc(rel_ready, 1)
                if r.within(BATCHES):
                    wait(dve, rank_ready, r.value(1, 1))
                    dve.tensor_tensor(first_free[:, :], count_ps, first_free[:, :], ALU.add).then_inc(free_ready, 1)
                    for kk in range(TOP_K):
                        dve.tensor_tensor(picked[:, kk * NT:(kk + 1) * NT, :], chosen[:, kk], rank[:, :, :],
                                          ALU.mult).then_inc(picked_ready, 1)
                if b.within(BATCHES):
                    wait(dve, rstd2_ready, b.value(1, 1))
                    wait(dve, xn2_ready, b.value(NT))
                    dve.scalar_tensor_tensor(shift2[:, :], mean2[:, :, 0], -1.0, rstd2[:, :],
                                             ALU.mult, ALU.mult).then_inc(shift2_ready, 1)
                if t_.within(BATCHES):
                    wait(dve, xnthi_ready, t_.value(1, 1))
                    dve.tensor_tensor(xnt_lo[:, q], xnt_ps, xnt_hi[:, q], ALU.subtract).then_inc(xntlo_ready, 1)
                if r.within(BATCHES):
                    wait(dve, picked_ready, r.value(TOP_K, TOP_K))
                    dve.tensor_reduce(row[:, :], picked[:, :, :], AX_X, ALU.add).then_inc(row_ready, 1)
                    wait(dve, row_ready, r.value(1, 1))
                    wait(dve, id_ready, r.value(TOP_K, TOP_K))
                    dve.tensor_scalar(row_u[:, r.place(ER), :], row[:, :], spare_row[:, 0:1], None,
                                      ALU.add).then_inc(rowu_ready, 1)
                if m.within(BATCHES):
                    wait(dve, relsq_ready, m.value(1, 1))
                    wait(dve, norm_done, m.value())
                    dve.tensor_tensor(sq_sum[:, :], rel_sq[:, 0, :], rel_sq[:, 1, :], ALU.add) \
                        .then_inc(sqsum_ready, 1)
                if r.within(BATCHES):
                    wait(dve, up_hi_ready, r.value(1, 1))
                    dve.tensor_tensor(up_piece(r, up_lo), up_piece(r, up_raw), up_piece(r, up_hi), ALU.subtract) \
                        .then_inc(up_lo_ready, 1)
                if k.i is None:
                    for e in down_splits.get(k.base, []):
                        lo_of_down(e)

            graph_steps(dve, step)

            n = 0
            dve.wait_ge(free_ready, BATCHES + 1)
            dve.tensor_tensor(count_i[:, :], first_free[:, :], start_row[:, :], ALU.subtract).then_inc(plan, 1)
            dve.wait_ge(plan, n + 1)
            dve.tensor_scalar(count_i[:, :], count_i[:, :], P - 1, None, ALU.add).then_inc(plan, 1)
            dve.wait_ge(plan, n + 2)
            dve.tensor_scalar(slots_i[:, :], count_i[:, :], P.bit_length() - 1, None,
                              ALU.logical_shift_right).then_inc(plan, 1)
            dve.wait_ge(plan, n + 3)
            dve.tensor_copy(slots_of[:, :], slots_i[:, :]).then_inc(plan, 1)
            dve.wait_ge(plan, n + 4)
            dve.tensor_tensor_scan(slots_end[:, :], all_ones[:, :], slots_of[:, :], 0.0, ALU.mult, ALU.add) \
                .then_inc(plan, 1)
            dve.tensor_scalar(slot_gap[:, :], slots_of[:, :], -1.0, float(TILES), ALU.mult, ALU.add).then_inc(plan, 1)
            dve.wait_ge(plan, n + 6)
            for j in range(2):
                dve.tensor_scalar(past[:, j, :], slots_end[:, :], slot_no[:, j:j + 1], None, ALU.is_le) \
                    .then_inc(plan, 1)
            dve.wait_ge(plan, n + 8)
            dve.tensor_tensor(skipped[:, :, :], past[:, :, :],
                              slot_gap[:, :].unsqueeze(1).to_broadcast([P, 2, EXPERTS]), ALU.mult).then_inc(plan, 1)
            dve.wait_ge(plan, n + 9)
            dve.tensor_reduce(table_row[:, :], skipped[:, :, :], AX_X, ALU.add).then_inc(plan, 1)
            dve.wait_ge(plan, n + 10)
            dve.tensor_tensor(table_row_u[:, :], table_row[:, :], slot_no[:, :], ALU.add).then_inc(tablerow_ready, 1)
            dve.tensor_scalar(expert_f[:, :], slot_free[:, :], slots_end[0:1, 0:1], None, ALU.is_ge) \
                .then_inc(plan, 1)
            for e in range(1, EXPERTS):
                dve.wait_ge(plan, n + 10 + e)
                dve.scalar_tensor_tensor(expert_f[:, :], slot_free[:, :], slots_end[0:1, e:e + 1], expert_f[:, :],
                                         ALU.is_ge, ALU.add).then_inc(plan, 1)
            n += 10 + EXPERTS
            dve.wait_ge(plan, n)
            dve.tensor_scalar(weights_at[:, :], expert_f[:, :], float(EXPERTS - 1), float(WEIGHTS), ALU.min, ALU.mult) \
                .then_inc(experts_ready, 1)
            for e in range(2, EXPERTS - 3):
                lo_of_down(e)

            def name_tokens(c, ps, is_pad, at):
                dve.wait_ge(byslot_done, c + 1)
                dve.tensor_scalar(is_pad[:, :], ps[0], 0.0, pad_id[:, 0:1], ALU.is_equal, ALU.mult) \
                    .then_inc(plan, 1)
                dve.wait_ge(plan, n + c + 1)
                dve.scalar_tensor_tensor(ids[:, at], ps[0], -1.0, is_pad[:, :], ALU.add, ALU.add) \
                    .then_inc(ids_ready, 1)

            name_tokens(0, byslot1_ps, is_pad1, slice(0, P))
            dve.wait_ge(ids_ready, 1)
            for e in range(EXPERTS - 3, EXPERTS):
                lo_of_down(e)

            def transposed(s):
                wait(dve, xgthi_ready, s.value(1, 1))
                dve.tensor_tensor(xgt_lo[:, :, :], xgt_ps, xgt_hi[:, :, :], ALU.subtract).then_inc(xgtlo_ready, 1)

            transposed(Index(0))

            def expert_step(s):
                d = s - 1
                if d.within(SLOTS):
                    wait(dve, hthi_ready, d.value(1, 1))
                    dve.tensor_tensor(ht_lo[:, :, :], ht_ps, ht_hi[:, :, :], ALU.subtract).then_inc(htlo_ready, 1)
                if s.within(SLOTS):
                    wait(dve, up3_done, s.value(1, 1))
                    wait(dve, silu_ready, s.value(1, 1))
                    dve.tensor_tensor(h[:, :], up3_ps[:, :], h[:, :], ALU.mult).then_inc(h_ready, 1)
                if (s + 1).within(SLOTS):
                    transposed(s + 1)
                if s.i is None and s.base == 0:
                    dve.wait_ge(gates_ready, 2)
                    name_tokens(1, byslot2_ps, is_pad2, slice(P, SLOTS))

            expert_steps(dve, expert_step)

        @block.tensor
        def _(pe):
            def product(out_ps, left, right, first, last):
                for i, (a, b) in enumerate(((0, 0), (0, 1), (1, 0))):
                    mm = pe.matmul(out_ps, left[a], right[b], start=(first and i == 0), stop=(last and i == 2))
                return mm

            pe.wait_ge(ident_made, 1)
            pe.wait_ge(wqk_loaded, 32)
            for c in range(DC):
                for e in range(DC):
                    mm = pe.matmul(g_ps[:, c, :], wq_sb[:, e, c * P:(c + 1) * P], wk_sb[:, e, :],
                                   start=(e == 0), stop=(e == DC - 1))
            mm.then_inc(a_done, 1)
            pe.wait_ge(wv_loaded, 16)
            for c in range(DC):
                for e in range(DC):
                    mm = pe.transpose(v_ps[:, c, e * P:(e + 1) * P], wv_sb[:, e, c * P:(c + 1) * P], ident[:, :])
            mm.then_inc(wvt_done, 1)

            def step(k):
                m = k - 2
                if m.within(BATCHES):
                    q = m.place(2)
                    if m.i is None and m.base == 0:
                        pe.wait_ge(a_hi_ready, 1)
                        pe.wait_ge(a_lo_ready, 1)
                        pe.wait_ge(wvt_hi_ready, 1)
                        pe.wait_ge(wvt_lo_ready, 1)
                    wait(pe, xntlo_ready, m.value(1, 1))
                    wait(pe, glo_ready, m.value())
                    for c in range(DC):
                        cols = slice(c * P, (c + 1) * P)
                        for e in range(DC):
                            mm = product(g_ps[:, c, :], (at_hi[:, e, cols], at_lo[:, e, cols]),
                                         (xnt_hi[:, q, e, :], xnt_lo[:, q, e, :]), e == 0, e == DC - 1)
                    mm.then_inc(g_done, 1)
                    wait(pe, v_ready, m.value())
                    for t in range(NT):
                        for e in range(DC):
                            cols = slice(t * P, (t + 1) * P)
                            mm = product(v_ps[:, t, :], (xnt_hi[:, q, e, cols], xnt_lo[:, q, e, cols]),
                                         (wvt_hi[:, e, :], wvt_lo[:, e, :]), e == 0, e == DC - 1)
                    mm.then_inc(v_done, 1)
                b = k - 4
                if b.within(BATCHES):
                    wait(pe, xn2_ready, b.value(NT, NT))
                    wait(pe, xn2t_ready, b.value())
                    for t in range(NT):
                        for c in range(DC):
                            mm = pe.transpose(xn2t_ps[:, c, t * P:(t + 1) * P],
                                              xn2[:, b.place(2), t, c * P:(c + 1) * P], ident[:, :])
                    mm.then_inc(xn2t_done, 1)
                r = k - 5
                if r.within(BATCHES):
                    if r.i is None and r.base == 0:
                        pe.wait_ge(before_made, 1)
                        pe.wait_ge(consts_made, 2)
                    wait(pe, either_ready, r.value(1, 1))
                    pe.matmul(rank_ps[:, 0, :], before[:, :], either[:, 0, :], start=True, stop=True)
                    pe.matmul(rank_ps[:, 1, :], before[:, :], either[:, 1, :], start=True, stop=False)
                    pe.matmul(rank_ps[:, 1, :], ones[:, :], either[:, 0, :], start=False, stop=True)
                    pe.matmul(count_ps, ones[:, :], either[:, 0, :], start=True, stop=False)
                    pe.matmul(count_ps, ones[:, :], either[:, 1, :], start=False, stop=True).then_inc(prefix_done, 1)
                if m.within(BATCHES):
                    wait(pe, glo_ready, m.value(1, 1))
                    wait(pe, rel_ready, m.value())
                    for t in range(NT):
                        for e in range(DC):
                            cols = slice(t * P, (t + 1) * P)
                            mm = product(rel_ps[:, t, :], (xnt_hi[:, q, e, cols], xnt_lo[:, q, e, cols]),
                                         (g_hi[:, e, :], g_lo[:, e, :]), e == 0, e == DC - 1)
                    mm.then_inc(rel_done, 1)
                f = k - 1
                if f.within(BATCHES):
                    wait(pe, xn_ready, f.value(NT, NT))
                    wait(pe, xntlo_ready, f.value())
                    for t in range(NT):
                        for c in range(DC):
                            mm = pe.transpose(xnt_ps[:, c, t * P:(t + 1) * P],
                                              xn[:, f.place(2), t, c * P:(c + 1) * P], ident[:, :])
                    mm.then_inc(xnt_done, 1)
                if b.within(BATCHES):
                    if b.i is None and b.base == 0:
                        pe.wait_ge(gate_w_loaded, 32)
                    wait(pe, xn2t_ready, b.value(1, 1))
                    wait(pe, logit_ready, b.value())
                    for t in range(NT):
                        for e in range(DC):
                            mm = pe.matmul(logit_ps[:, t, :], xn2_t[:, e, t * P:(t + 1) * P], wg_sb[:, e, :],
                                           start=(e == 0), stop=(e == DC - 1))
                    mm.then_inc(logit_done, 1)
                if m.within(BATCHES):
                    wait(pe, rel_ready, m.value(1, 1))
                    wait(pe, v_ready, m.value(1, 1))
                    wait(pe, x1_ready, m.value(NT))
                    for t in range(NT):
                        for e in range(NT):
                            mm = pe.matmul(mix_ps[:, t, :], rel[:, e, t * P:(t + 1) * P], v[:, e, :],
                                           start=(e == 0), stop=(e == NT - 1))
                    mm.then_inc(mix_done, 1)
                    wait(pe, sqsum_ready, m.value(1, 1))
                    wait(pe, normsq_ready, m.value())
                    if r.within(BATCHES):
                        wait(pe, free_ready, r.value(1, 2))
                    for t in range(NT):
                        mm = pe.matmul(norm_ps[:, t:t + 1], sq_sum[:, t * P:(t + 1) * P], ones_col[:, :],
                                       start=True, stop=True)
                    mm.then_inc(norm_done, 1)

            graph_steps(pe, step)

            def by_row(n, of, loaded, ps):
                for j in range(len(tables)):
                    pe.wait_ge(loaded[j], 16)
                    for c in range(2):
                        mm = pe.matmul(ps[c], of[:, j, :, c], ident[0:n, 0:n],
                                       start=(j == 0), stop=(j == len(tables) - 1))
                mm.then_inc(byslot_done, 1)

            pe.wait_ge(xn2t_ready, BATCHES)
            pe.wait_ge(normsq_ready, BATCHES)
            pe.wait_ge(free_ready, BATCHES + 1)
            by_row(P, by_slot1, byslot1_loaded, byslot1_ps)
            pe.wait_ge(experts_ready, 1)
            pe.wait_ge(up_lo_ready, BATCHES)
            pe.wait_ge(rel_ready, BATCHES)
            pe.wait_ge(v_ready, BATCHES)
            pe.wait_ge(x1_ready, BATCHES * NT)

            down_at_w, up_at_w, next_at_w = (pe.alloc_register(n) for n in ("down_at_w", "up_at_w", "next_at_w"))

            def read_next(s):
                pe.reg_load(next_at_w, weights_at[0:1, bass.ds(s.value(), 1)])

            def transpose_x(s):
                wait(pe, xg_loaded[s.place(2)], s.before(2) * 16 + 16)
                wait(pe, xgtlo_ready, s.value())
                for c in range(DC):
                    mm = pe.transpose(xgt_ps[:, c, :], xg[:, s.place(2), c * P:(c + 1) * P], ident[:, :])
                mm.then_inc(xgt_done, 1)

            read_next(Index(0))
            pe.reg_mov(up_at_w, 0)
            transpose_x(Index(0))

            def expert_step(s):
                d = s - 1
                pe.reg_mov(down_at_w, up_at_w)
                pe.reg_mov(up_at_w, next_at_w)
                if d.within(SLOTS):
                    wait(pe, h_ready, d.value(1, 1))
                    wait(pe, htlo_ready, d.value())
                    for c in range(HC):
                        mm = pe.transpose(ht_ps[:, c, :], h[:, c * P:(c + 1) * P], ident[:, :])
                    mm.then_inc(ht_done, 1)
                if s.within(SLOTS):
                    w = pe.snap(up_at_w, min_val=0, max_val=(EXPERTS - 1) * DC * HID)
                    wait(pe, xgtlo_ready, s.value(1, 1))
                    wait(pe, silu_ready, s.value())
                    for c in range(DC):
                        cols = bass.ds(w + c * HID, HID)
                        mm = product(up1_ps[:, :], (xgt_hi[:, c, :], xgt_lo[:, c, :]), (up_hi[:, cols], up_lo[:, cols]),
                                     c == 0, c == DC - 1)
                    mm.then_inc(up1_done, 1)
                    wait(pe, h_ready, s.value())
                    for c in range(DC):
                        cols = bass.ds(w + (EXPERTS * WEIGHTS + c * HID), HID)
                        mm = product(up3_ps[:, :], (xgt_hi[:, c, :], xgt_lo[:, c, :]), (up_hi[:, cols], up_lo[:, cols]),
                                     c == 0, c == DC - 1)
                    mm.then_inc(up3_done, 1)
                if (s + 1).within(SLOTS):
                    transpose_x(s + 1)
                    read_next(s + 1)
                if s.i is None and s.base == 0:
                    pe.wait_ge(logit_ready, BATCHES)
                    pe.wait_ge(gates_ready, 1)
                    by_row(S2, by_slot2, byslot2_loaded, byslot2_ps)
                if d.within(SLOTS):
                    w = pe.snap(down_at_w, min_val=0, max_val=(EXPERTS - 1) * HC * D)
                    if d.i is None and d.base == 0:
                        pe.wait_ge(down_lo_ready, EXPERTS)
                    wait(pe, htlo_ready, d.value(1, 1))
                    wait(pe, y_ready, d.value())
                    for c in range(HC):
                        cols = bass.ds(w + c * D, D)
                        mm = product(down_ps, (ht_hi[:, c, :], ht_lo[:, c, :]), (w2_hi[:, cols], w2_lo[:, cols]),
                                     c == 0, c == HC - 1)
                    mm.then_inc(down_done, 1)

            expert_steps(pe, expert_step)


def kernel(x, adj, L0_gnn_Wq, L0_gnn_Wk, L0_gnn_Wv, L0_ffn_Wg, L0_ffn_bg, L0_ffn_W1, L0_ffn_W3, L0_ffn_W2):
    import numpy as np
    import concourse.bacc as bacc
    from concourse.bass_utils import run_bass_kernel_spmd

    given = {"x": x, "adj": adj, "w_q": L0_gnn_Wq, "w_k": L0_gnn_Wk, "w_v": L0_gnn_Wv, "w_gate": L0_ffn_Wg,
             "b_gate": L0_ffn_bg, "w_1": L0_ffn_W1, "w_3": L0_ffn_W3, "w_2": L0_ffn_W2}
    nc = bacc.Bacc("TRN2", target_bir_lowering=False, num_devices=1)
    arrays, args = {}, []
    for name, a in given.items():
        a = np.ascontiguousarray(a)
        arrays[f"in_{name}"] = a
        args.append(nc.dram_tensor(f"in_{name}", a.shape, mybir.dt.from_np(a.dtype), kind="ExternalInput").ap())
    batches, nodes, d = x.shape
    out = nc.dram_tensor("out", (batches * nodes + P, d), F32, kind="ExternalOutput").ap()
    graph_and_experts(nc, *args, out)
    r = run_bass_kernel_spmd(nc, [arrays], core_ids=[0])
    return r.results[0]["out"][:batches * nodes].reshape(batches, nodes, d)
```
